# Optimizing a Trainium2 kernel written in Bass

```python
import numpy as np
import jax
import jax.numpy as jnp

def _softmax(x, axis=-1):
    return jax.nn.softmax(x, axis=axis)

def _gelu(x):
    return jax.nn.gelu(x, approximate=True)

def _silu(x):
    return jax.nn.silu(x)

def _sigmoid(x):
    return jax.nn.sigmoid(x)

def _layernorm(x, axis=-1, eps=1e-05):
    m = jnp.mean(x, axis=axis, keepdims=True)
    v = jnp.var(x, axis=axis, keepdims=True)
    return (x - m) / jnp.sqrt(v + eps)

def _scatter_add(tgt, idx, src, axis=0):
    return tgt.at[idx].add(src)

def _segment_sum(src, seg, n):
    return jax.ops.segment_sum(src, seg, n)
kernel_name = 'mk_xattn_ffn_d1_seqx_r4_8e6f6d'

def setup_inputs(seed: int=0):
    np.random.seed(seed)
    _w = jnp.asarray

    def _rec_inputs():
        import jax
        import jax.numpy as jnp
        _rk = jax.random.key(seed)
        x = -0.000125 + 0.9999 * jax.random.normal(jax.random.fold_in(_rk, 1), (2, 1024, 256), jnp.float32)
        _lenS = 1024 - jax.random.randint(jax.random.fold_in(_rk, 7), (2,), 0, max(1, 1024 // 4) + 1, jnp.int32)
        _lenS2 = 77 - jax.random.randint(jax.random.fold_in(_rk, 8), (2,), 0, max(1, 77 // 4) + 1, jnp.int32)
        _ctx_1024P = jax.random.normal(jax.random.fold_in(_rk, 11), (2, 16, 256), jnp.float32)
        _ctx_1024c = jax.random.dirichlet(jax.random.fold_in(_rk, 511), 0.3 * jnp.ones((16,), jnp.float32), (2, 77))
        _ctx_1024t = jnp.einsum('bsk,bkd->bsd', _ctx_1024c, _ctx_1024P)
        _ctx_1024t = _ctx_1024t * jax.lax.rsqrt(jnp.mean(jnp.square(_ctx_1024t)) + 1e-12) * 0.953939
        ctx_1024 = -1.52775e-05 + 0.999936 * (_ctx_1024t + 0.3 * jax.random.normal(jax.random.fold_in(_rk, 611), (2, 77, 256), jnp.float32))
        return (x, ctx_1024)
    x, ctx_1024 = _rec_inputs()

    def _L0_xattn_setup():
        import jax, jax.numpy as jnp
        import numpy as np
        B, LP, LQ, H = (16, 512, 512, 256)
        key = jax.random.key(seed)
        k1, k2, k3 = jax.random.split(key, 3)
        proj_p = jax.random.normal(k1, (B, LP, H), dtype=jnp.float32)
        proj_q = jax.random.normal(k2, (B, LQ, H), dtype=jnp.float32)
        W = jax.random.normal(k3, (H, H), dtype=jnp.float32) * (1.0 / np.sqrt(H))
        b = jnp.zeros((H,), dtype=jnp.float32)
        return {'proj_p': proj_p, 'proj_q': proj_q, 'W': W, 'b': b}
    _L0_xattn_all = _L0_xattn_setup()
    _L0_xattn_in = {k: v for k, v in _L0_xattn_all.items() if k in ('W', 'b')}
    del _L0_xattn_all

    def _L0_ffn_setup():
        import jax, jax.numpy as jnp
        import numpy as np
        from jax import lax
        T, B, I, M, O = (64, 64, 256, 256, 256)

        def _xavier(key, shape):
            fan_out, fan_in = shape
            limit = float(np.sqrt(6.0 / (fan_in + fan_out)))
            return jax.random.uniform(key, shape, jnp.float32, -limit, limit)
        key = jax.random.key(seed)
        ks = jax.random.split(key, 9)
        x = jax.random.normal(ks[0], (T, B, I), jnp.float32)
        return {'x': x, 'wf': _xavier(ks[1], (M, I)), 'uf': _xavier(ks[2], (M, M)), 'bf': jnp.zeros((M,), jnp.float32), 'wi': _xavier(ks[3], (M, I)), 'ui': _xavier(ks[4], (M, M)), 'bi': jnp.zeros((M,), jnp.float32), 'wc': _xavier(ks[5], (M, I)), 'uc': _xavier(ks[6], (M, M)), 'bc': jnp.zeros((M,), jnp.float32), 'wo': _xavier(ks[7], (O, I)), 'uo': _xavier(ks[8], (O, M)), 'bo': jnp.zeros((O,), jnp.float32), 'in_c': jnp.zeros((M,), jnp.float32)}
    _L0_ffn_all = _L0_ffn_setup()
    _L0_ffn_in = {k: v for k, v in _L0_ffn_all.items() if k in ('wf', 'uf', 'bf', 'wi', 'ui', 'bi', 'wc', 'uc', 'bc', 'wo', 'uo', 'bo', 'in_c')}
    del _L0_ffn_all
    return {'x': x, 'ctx_1024': ctx_1024, 'L0_xattn_W': _L0_xattn_in['W'], 'L0_xattn_b': _L0_xattn_in['b'], 'L0_ffn_wf': _L0_ffn_in['wf'], 'L0_ffn_uf': _L0_ffn_in['uf'], 'L0_ffn_bf': _L0_ffn_in['bf'], 'L0_ffn_wi': _L0_ffn_in['wi'], 'L0_ffn_ui': _L0_ffn_in['ui'], 'L0_ffn_bi': _L0_ffn_in['bi'], 'L0_ffn_wc': _L0_ffn_in['wc'], 'L0_ffn_uc': _L0_ffn_in['uc'], 'L0_ffn_bc': _L0_ffn_in['bc'], 'L0_ffn_wo': _L0_ffn_in['wo'], 'L0_ffn_uo': _L0_ffn_in['uo'], 'L0_ffn_bo': _L0_ffn_in['bo'], 'L0_ffn_in_c': _L0_ffn_in['in_c']}

def reference(x, ctx_1024, L0_xattn_W, L0_xattn_b, L0_ffn_wf, L0_ffn_uf, L0_ffn_bf, L0_ffn_wi, L0_ffn_ui, L0_ffn_bi, L0_ffn_wc, L0_ffn_uc, L0_ffn_bc, L0_ffn_wo, L0_ffn_uo, L0_ffn_bo, L0_ffn_in_c):
    import jax
    import jax.numpy as jnp

    def _L0_xattn_ref(proj_p, proj_q, W, b):
        import jax, jax.numpy as jnp
        import numpy as np
        B, LP, LQ, H = (16, 512, 512, 256)
        trans_q = jnp.einsum('bqh,oh->bqo', proj_q, W) + b
        att_weights = jnp.einsum('bph,bqh->bpq', proj_p, trans_q)
        att_norm = jax.nn.softmax(att_weights, axis=-1)
        att_vec = jnp.einsum('bpq,bqh->bph', att_norm, proj_q)
        out = jax.nn.relu(jnp.einsum('bph,oh->bpo', att_vec, W) + b)
        return out

    def _L0_ffn_ref(x, wf, uf, bf, wi, ui, bi, wc, uc, bc, wo, uo, bo, in_c):
        import jax, jax.numpy as jnp
        import numpy as np
        from jax import lax
        T, B, I, M, O = (64, 64, 256, 256, 256)

        def _xavier(key, shape):
            fan_out, fan_in = shape
            limit = float(np.sqrt(6.0 / (fan_in + fan_out)))
            return jax.random.uniform(key, shape, jnp.float32, -limit, limit)
        batch = x.shape[1]
        c0 = jnp.broadcast_to(in_c, (batch, in_c.shape[0]))

        def step(c, xt):
            ft = jax.nn.sigmoid(xt @ wf.T + c @ uf.T + bf)
            it = jax.nn.sigmoid(xt @ wi.T + c @ ui.T + bi)
            gt = jnp.tanh(xt @ wc.T + c @ uc.T + bc)
            c = ft * c + it * gt
            return (c, None)
        c_final, _ = lax.scan(step, c0, x)
        h = jnp.tanh(jnp.einsum('tbi,oi->tbo', x, wo) + c_final @ uo.T + bo)
        return h
    x = x + _L0_xattn_ref(_layernorm(x, axis=-1), ctx_1024, L0_xattn_W, L0_xattn_b)
    x = x + _L0_ffn_ref(_layernorm(x, axis=-1), L0_ffn_wf, L0_ffn_uf, L0_ffn_bf, L0_ffn_wi, L0_ffn_ui, L0_ffn_bi, L0_ffn_wc, L0_ffn_uc, L0_ffn_bc, L0_ffn_wo, L0_ffn_uo, L0_ffn_bo, L0_ffn_in_c)
    return x

_drawn_inputs = setup_inputs


def setup_inputs(seed=0):
    import zlib

    import numpy as np

    out = dict(_drawn_inputs(seed))
    spreads = {'L0_xattn_b': (0.0, 0.1),
     'L0_ffn_bf': (0.0, 0.8),
     'L0_ffn_bi': (0.0, 0.8),
     'L0_ffn_bc': (0.0, 0.361),
     'L0_ffn_bo': (0.0, 0.1),
     'L0_ffn_in_c': (0.0, 0.377)}
    factors = {'L0_ffn_uf': 5.111, 'L0_ffn_ui': 2.726}
    for name, (base, spread) in spreads.items():
        noise = np.random.default_rng([zlib.crc32(name.encode()), seed]).standard_normal(out[name].shape)
        drawn = base * np.exp(spread * noise) if base else spread * noise
        out[name] = jnp.asarray(drawn.astype(out[name].dtype))
    for name, factor in factors.items():
        out[name] = (out[name] * factor).astype(out[name].dtype)
    return out
```

```python
from contextlib import ExitStack

import concourse.bass as bass
from concourse import mybir

F32 = mybir.dt.float32
F32R = mybir.dt.float32r
ALU = mybir.AluOpType
ACT = mybir.ActivationFunctionType
AX = mybir.AxisListType

P = 128
STEPS, ROWS, D = 2, 1024, 256
KEYS = 77
KC = D // P
GROUPS = 2
SLAB = ROWS // GROUPS
TILES = SLAB // P
SLABS = GROUPS * STEPS
EPS = 1e-5
GATES = 3
HEAD = 3
RING = 4
V_GATE, V_ATTN, V_C0, V_COUNT = 0, GATES * KC, GATES * KC + KC, GATES * KC + 2 * KC


def build(nc, x, xT, ctx_w, wT, uT, vecs, bo, out):
    with ExitStack() as ctx:
        def sb(name, shape, dt=F32):
            return ctx.enter_context(nc.sbuf_tensor(name, shape, dt))

        def psum(name):
            return ctx.enter_context(nc.psum_tensor(name, [P, 512], F32))

        def sem(name):
            return ctx.enter_context(nc.semaphore(name))

        X = sb("X", [P, SLABS, TILES, D])
        XT = sb("XT", [P, 2, KC, SLAB])
        CW = sb("CW", [P, KC, D + STEPS * KEYS])
        W = sb("W", [P, KC, HEAD + 1, D])
        U = sb("U", [P, KC, HEAD + 1, D])
        W_hi = sb("W_hi", [P, KC, HEAD + 1, D], F32R)
        W_lo = sb("W_lo", [P, KC, HEAD + 1, D], F32R)
        U_half = sb("U_half", [P, KC, HEAD + 1, D])
        U_hi = sb("U_hi", [P, KC, HEAD + 1, D], F32R)
        U_lo = sb("U_lo", [P, KC, HEAD + 1, D], F32R)
        vec = sb("vec", [P, V_COUNT])
        bo_rows = sb("bo_rows", [33, STEPS * D])
        bo_hilo = sb("bo_hilo", [33, STEPS * D], F32R)
        ones_f = sb("ones_f", [33, P])
        ones_r = sb("ones_r", [33, P], F32R)
        ident = sb("ident", [P, P])
        mean_w = sb("mean_w", [P, P])
        neg_half = sb("neg_half", [P, TILES])
        T_T = sb("T_T", [P, KC, STEPS * KEYS])
        Tc_T = sb("Tc_T", [P, KC, STEPS * KEYS])
        T_rows = sb("T_rows", [KEYS, STEPS, D])
        bias0 = sb("bias0", [P, GATES * KC])
        bias1 = sb("bias1", [P, GATES * KC])
        bias_u = sb("bias_u", [P, GATES * KC])
        st1 = sb("st1", [P, SLABS, TILES, 6])
        mv1 = sb("mv1", [P, SLABS, TILES, 2])
        ve1 = sb("ve1", [P, SLABS, TILES])
        rstd1 = sb("rstd1", [P, SLABS, TILES])
        st2 = sb("st2", [P, SLABS, TILES, 6])
        mv2 = sb("mv2", [P, SLABS, TILES, 2])
        ve2 = sb("ve2", [P, SLABS, TILES])
        rstd2 = sb("rstd2", [P, SLABS, TILES])
        row_max = sb("row_max", [P, SLABS, TILES])
        exp_bias = sb("exp_bias", [P, SLABS, TILES])
        row_sum = sb("row_sum", [P, SLABS, TILES])
        row_rec = sb("row_rec", [P, SLABS, TILES])
        probs = sb("probs", [P, SLABS, TILES, KEYS])
        probs_n = sb("probs_n", [P, SLABS, TILES, KEYS])
        probs_T = sb("probs_T", [KEYS, 2, SLAB])
        H = sb("H", [P, 2, TILES, D])
        HT_hi = sb("HT_hi", [P, SLABS, KC, SLAB], F32R)
        HT_lo = sb("HT_lo", [P, SLABS, KC, SLAB], F32R)
        gate = sb("gate", [P, GATES, KC, SLAB])
        keep = sb("keep", [P, KC, SLAB])
        add = sb("add", [P, KC, SLAB])
        C = sb("C", [P, 2, KC, SLAB])
        C_hi = sb("C_hi", [P, 2, KC, SLAB], F32R)
        C_lo = sb("C_lo", [P, 2, KC, SLAB], F32R)
        head = sb("head", [P, TILES, STEPS, D])
        warm = sb("warm", [P, 1])

        p_scores = psum("p_scores")
        p_probsT = psum("p_probsT")
        p_slab = [psum(f"p_slab{k}") for k in range(2)]
        p_ring = [psum(f"p_ring{k}") for k in range(RING)]

        l_cw, l_vec, l_bo, l_w, l_u = (sem(n) for n in ("l_cw", "l_vec", "l_bo", "l_w", "l_u"))
        l_x = [sem(f"l_x{s}") for s in range(SLABS)]
        l_xT = [sem(f"l_xT{s}") for s in range(SLABS)]
        stored = [sem(f"stored{j}") for j in range(TILES)]
        s_warm = sem("s_warm")
        s_zero = sem("s_zero")
        s_ident = sem("s_ident")
        s_ones = sem("s_ones")
        s_whi = sem("s_whi")
        s_wlo = sem("s_wlo")
        s_uhalf = sem("s_uhalf")
        s_uhi = sem("s_uhi")
        s_ulo = sem("s_ulo")
        s_bohi = sem("s_bohi")
        s_bolo = sem("s_bolo")
        s_tps = sem("s_tps")
        s_tT = sem("s_tT")
        s_tmean = sem("s_tmean")
        s_trows = sem("s_trows")
        s_tc = sem("s_tc")
        s_trc = sem("s_trc")
        s_bps = sem("s_bps")
        s_bu = sem("s_bu")
        s_bias = sem("s_bias")
        s_st1, s_mv1, s_ve1, s_rstd1 = (sem(n) for n in ("s_st1", "s_mv1", "s_ve1", "s_rstd1"))
        s_scores = sem("s_scores")
        s_max = sem("s_max")
        s_ebias = sem("s_ebias")
        s_exp = sem("s_exp")
        s_rec = sem("s_rec")
        s_pn = sem("s_pn")
        s_pT = sem("s_pT")
        s_pTc = sem("s_pTc")
        s_att = sem("s_att")
        s_x1 = sem("s_x1")
        s_st2, s_mv2, s_ve2, s_rstd2 = (sem(n) for n in ("s_st2", "s_mv2", "s_ve2", "s_rstd2"))
        s_h = sem("s_h")
        s_hT = sem("s_hT")
        s_hhi = sem("s_hhi")
        s_hlo = sem("s_hlo")
        s_ring = sem("s_ring")
        s_act = sem("s_act")
        s_keep = sem("s_keep")
        s_add = sem("s_add")
        s_c = sem("s_c")
        s_chi = sem("s_chi")
        s_clo = sem("s_clo")
        s_y = sem("s_y")

        first = {("gates", 0, 0): 0, ("gates", 0, 1): 6, ("gates", 1, 0): 12, ("head", 0): 18,
                 ("gates", 1, 1): 22, ("head", 1): 28}

        def gate_of(i):
            return i // GATES, i % GATES

        block = ctx.enter_context(nc.Block())

        @block.sync
        def _(sp):
            sp.dma_start(CW[:], ctx_w).then_inc(l_cw, 16)
            sp.dma_start(vec[:], vecs).then_inc(l_vec, 16)

            def load_slab(s):
                if s >= 2:
                    sp.wait_ge(s_scores, s - 1)
                sp.dma_start(XT[:, s % 2], xT[:, s]).then_inc(l_xT[s], 16)
                g, t = s // STEPS, s % STEPS
                rows = x[t, g * SLAB:(g + 1) * SLAB, :].rearrange("(p j) d -> p j d", j=TILES)
                sp.dma_start(X[:, s], rows).then_inc(l_x[s], 16)

            load_slab(0)
            sp.dma_start(W[:], wT).then_inc(l_w, 16)
            load_slab(1)
            sp.dma_start(U[:], uT).then_inc(l_u, 16)
            sp.wait_ge(s_zero, 1)
            for t in range(STEPS):
                for p in (0, 32):
                    sp.dma_start(bo_rows[p:p + 1, t * D:(t + 1) * D], bo).then_inc(l_bo, 16)
            load_slab(2)
            load_slab(3)
            for g in range(GROUPS):
                for j in range(TILES):
                    sp.wait_ge(s_y, g * TILES + j + 1)
                    rows = out[:, g * SLAB:(g + 1) * SLAB, :].rearrange("t (p j) d -> p j t d", j=TILES)
                    sp.dma_start(rows[:, j], X[:, STEPS * g:STEPS * (g + 1), j]).then_inc(stored[j], 16)
            for j in range(TILES):
                sp.wait_ge(stored[j], 16 * GROUPS)

        @block.gpsimd
        def _(pool):
            nc.gpsimd.memset(bo_rows[:], 0.0).then_inc(s_zero, 1)
            nc.gpsimd.memset(mean_w[:], 1.0 / D).then_inc(s_ones, 1)
            nc.gpsimd.memset(ident[:], 0.0).then_inc(s_zero, 1)
            pool.wait_ge(s_zero, 2)
            nc.gpsimd.affine_select(out=ident[:], in_=ident[:], compare_op=ALU.not_equal, fill=1.0, base=0,
                                    pattern=[[-1, P]], channel_multiplier=1).then_inc(s_ident, 1)
            nc.gpsimd.memset(neg_half[:], -0.5).then_inc(s_ones, 1)
            nc.gpsimd.memset(ones_f[:], 1.0).then_inc(s_ones, 1)
            pool.wait_ge(s_ones, 3)
            nc.gpsimd.tensor_copy(ones_r[:], ones_f[:]).then_inc(s_ones, 1)

            def deviation1(s):
                pool.wait_ge(s_mv1, TILES * (s + 1))
                nc.gpsimd.tensor_scalar(ve1[:, s], mv1[:, s, :, 1], EPS, 1.0, ALU.add, ALU.mult).then_inc(s_ve1, 1)
                pool.wait_ge(s_ve1, s + 1)
                nc.gpsimd.tensor_tensor(rstd1[:, s], ve1[:, s], neg_half[:], ALU.pow).then_inc(s_rstd1, 1)

            def deviation2(s):
                pool.wait_ge(s_mv2, TILES * (s + 1))
                nc.gpsimd.tensor_scalar(ve2[:, s], mv2[:, s, :, 1], EPS, 1.0, ALU.add, ALU.mult).then_inc(s_ve2, 1)
                pool.wait_ge(s_ve2, s + 1)
                nc.gpsimd.tensor_tensor(rstd2[:, s], ve2[:, s], neg_half[:], ALU.pow).then_inc(s_rstd2, 1)

            deviation1(0)
            deviation1(1)
            for k in range(KC):
                pool.wait_ge(s_whi, k + 1)
                nc.gpsimd.tensor_tensor(W_lo[:, k], W[:, k], W_hi[:, k].bitcast(F32), ALU.subtract).then_inc(s_wlo, 1)
            deviation2(0)
            pool.wait_ge(l_u, 16)
            for k in range(KC):
                nc.gpsimd.tensor_scalar(U_half[:, k], U[:, k], 0.5, 1.0, ALU.mult, ALU.mult).then_inc(s_uhalf, 1)
            for k in range(KC):
                pool.wait_ge(s_uhi, k + 1)
                pool.wait_ge(s_uhalf, k + 1)
                nc.gpsimd.tensor_tensor(U_lo[:, k], U_half[:, k], U_hi[:, k].bitcast(F32),
                                        ALU.subtract).then_inc(s_ulo, 1)
                if k == 0:
                    deviation2(1)
            for s in range(2, SLABS):
                deviation1(s)
            for s in range(2, SLABS):
                deviation2(s)

        @block.scalar
        def _(act):
            act.wait_ge(s_warm, 1)
            nc.scalar.activation(warm[:], warm[:], ACT.Exp).then_inc(s_warm, 1)

            def exponentials(s):
                act.wait_ge(s_ebias, s + 1)
                for j in range(TILES):
                    e = nc.scalar.activation(probs[:, s, j], p_scores[:, j * KEYS:(j + 1) * KEYS], ACT.Exp,
                                             bias=exp_bias[:, s, j:j + 1], scale=rstd1[:, s, j:j + 1],
                                             accum_out=row_sum[:, s, j:j + 1])
                    e.then_inc(s_exp, 1)

            def probs_T_copy(s):
                act.wait_ge(s_pT, s + 1)
                if s >= 2:
                    act.wait_ge(s_att, 2 * (s - 1))
                nc.scalar.copy(probs_T[:, s % 2], p_probsT[0:KEYS, :]).then_inc(s_pTc, 1)

            def h_hi(s):
                for k in range(KC):
                    act.wait_ge(s_hT, KC * s + k + 1)
                    nc.scalar.copy(HT_hi[:, s, k], p_slab[k][:]).then_inc(s_hhi, 1)

            def gate_tanh(g, t, i):
                n = first["gates", g, t] + i
                oc, q = gate_of(i)
                act.wait_ge(s_ring, n + 1)
                if (t, i) == (0, 0):
                    act.wait_ge(s_bias, 4)
                if (g, t) != (0, 0):
                    act.wait_ge(s_keep, 4 * g + 2 * t + oc - 1)
                    act.wait_ge(s_add, 4 * g + 2 * t + oc - 1)
                bias = (bias0, bias1)[t]
                c = q * KC + oc
                nc.scalar.activation(gate[:, q, oc], p_ring[n % RING][:], ACT.Tanh, bias=bias[:, c:c + 1],
                                     scale=1.0 if q == 2 else 0.5).then_inc(s_act, 1)

            def c_hi(g, t, oc):
                act.wait_ge(s_c, 4 * g + 2 * t + oc + 1)
                if g == 1 and t == 0:
                    act.wait_ge(s_ring, 12)
                if g == 1 and t == 1:
                    act.wait_ge(s_ring, 22)
                nc.scalar.copy(C_hi[:, t, oc], C[:, t, oc]).then_inc(s_chi, 1)

            def head_tanh(g, j):
                n = first["head", g] + j
                act.wait_ge(s_ring, n + 1)
                if g == 1:
                    act.wait_ge(s_y, j + 1)
                nc.scalar.activation(head[:, j].rearrange("p t d -> p (t d)"), p_ring[n % RING][:],
                                     ACT.Tanh).then_inc(s_act, 1)

            act.wait_ge(s_trows, 1)
            nc.scalar.copy(T_rows[:], p_slab[0][0:KEYS, :].rearrange("p (t d) -> p t d", t=STEPS)).then_inc(s_trc, 1)
            exponentials(0)
            act.wait_ge(l_w, 16)
            nc.scalar.copy(W_hi[:, 0], W[:, 0]).then_inc(s_whi, 1)
            probs_T_copy(0)
            nc.scalar.copy(W_hi[:, 1], W[:, 1]).then_inc(s_whi, 1)
            exponentials(1)
            probs_T_copy(1)
            act.wait_ge(l_u, 16)
            nc.scalar.mul(U_hi[:, 0], U[:, 0], 0.5).then_inc(s_uhi, 1)
            h_hi(0)
            nc.scalar.mul(U_hi[:, 1], U[:, 1], 0.5).then_inc(s_uhi, 1)
            act.wait_ge(l_bo, 16 * 4)
            nc.scalar.copy(bo_hilo[:], bo_rows[:]).then_inc(s_bohi, 1)
            gate_tanh(0, 0, 0)
            gate_tanh(0, 0, 1)
            exponentials(2)
            gate_tanh(0, 0, 2)
            gate_tanh(0, 0, 3)
            h_hi(1)
            c_hi(0, 0, 0)
            probs_T_copy(2)
            gate_tanh(0, 0, 4)
            gate_tanh(0, 0, 5)
            c_hi(0, 0, 1)
            gate_tanh(0, 1, 0)
            exponentials(3)
            gate_tanh(0, 1, 1)
            h_hi(2)
            gate_tanh(0, 1, 2)
            probs_T_copy(3)
            gate_tanh(0, 1, 3)
            gate_tanh(0, 1, 4)
            c_hi(0, 1, 0)
            gate_tanh(0, 1, 5)
            c_hi(0, 1, 1)
            for i in range(3):
                gate_tanh(1, 0, i)
            h_hi(3)
            for i in range(3, 5):
                gate_tanh(1, 0, i)
            c_hi(1, 0, 0)
            gate_tanh(1, 0, 5)
            c_hi(1, 0, 1)
            for j in range(TILES):
                head_tanh(0, j)
            for i in range(5):
                gate_tanh(1, 1, i)
            c_hi(1, 1, 0)
            gate_tanh(1, 1, 5)
            c_hi(1, 1, 1)
            for j in range(TILES):
                head_tanh(1, j)

        @block.vector
        def _(dve):
            nc.vector.memset(warm[:], 0.0).then_inc(s_warm, 1)

            def stats1(s):
                dve.wait_ge(l_x[s], 16)
                for j in range(TILES):
                    nc.vector.bn_stats(st1[:, s, j], X[:, s, j]).then_inc(s_st1, 1)
                for j in range(TILES):
                    dve.wait_ge(s_st1, TILES * s + j + 1)
                    nc.vector.bn_aggr(mv1[:, s, j], st1[:, s, j]).then_inc(s_mv1, 1)

            def score_max(s):
                dve.wait_ge(s_scores, s + 1)
                nc.vector.tensor_reduce(row_max[:, s], p_scores[:, 0:TILES * KEYS].rearrange("p (j k) -> p j k", j=TILES),
                                        AX.X, ALU.max).then_inc(s_max, 1)
                dve.wait_ge(s_max, s + 1)
                dve.wait_ge(s_rstd1, s + 1)
                nc.vector.scalar_tensor_tensor(exp_bias[:, s], row_max[:, s], -1.0, rstd1[:, s], ALU.mult,
                                               ALU.mult).then_inc(s_ebias, 1)

            def normalise(s):
                dve.wait_ge(s_exp, TILES * (s + 1))
                nc.vector.reciprocal(row_rec[:, s], row_sum[:, s]).then_inc(s_rec, 1)
                dve.wait_ge(s_rec, s + 1)
                rec = row_rec[:, s].unsqueeze(2).to_broadcast([P, TILES, KEYS])
                nc.vector.tensor_tensor(probs_n[:, s], probs[:, s], rec, ALU.mult).then_inc(s_pn, 1)

            def residual(s):
                for i in range(2):
                    dve.wait_ge(s_att, 2 * s + i + 1)
                    nc.vector.scalar_tensor_tensor(X[:, s, 2 * i:2 * i + 2],
                                                   p_slab[i][:].rearrange("p (j d) -> p j d", j=2), 0.0,
                                                   X[:, s, 2 * i:2 * i + 2], ALU.max, ALU.add).then_inc(s_x1, 1)
                for j in range(TILES):
                    dve.wait_ge(s_x1, 2 * s + j // 2 + 1)
                    nc.vector.bn_stats(st2[:, s, j], X[:, s, j]).then_inc(s_st2, 1)
                for j in range(TILES):
                    dve.wait_ge(s_st2, TILES * s + j + 1)
                    nc.vector.bn_aggr(mv2[:, s, j], st2[:, s, j]).then_inc(s_mv2, 1)

            def layernorm(s):
                dve.wait_ge(s_rstd2, s + 1)
                if s >= 2:
                    dve.wait_ge(s_hT, KC * (s - 1))
                for j in range(TILES):
                    nc.vector.tensor_scalar(H[:, s % 2, j], X[:, s, j], mv2[:, s, j, 0:1], rstd2[:, s, j:j + 1],
                                            ALU.subtract, ALU.mult).then_inc(s_h, 1)

            def h_lo(s):
                for k in range(KC):
                    dve.wait_ge(s_hhi, KC * s + k + 1)
                    nc.vector.tensor_tensor(HT_lo[:, s, k], p_slab[k][:], HT_hi[:, s, k].bitcast(F32),
                                            ALU.subtract).then_inc(s_hlo, 1)

            def state(g, t, oc):
                n = first["gates", g, t] + GATES * oc
                done = 4 * g + 2 * t + oc
                dve.wait_ge(s_act, n + 1)
                if done >= 2:
                    dve.wait_ge(s_c, done - 1)
                if t == 0:
                    nc.vector.tensor_scalar(keep[:, oc], gate[:, 0, oc], 1.0, vec[:, V_C0 + oc:V_C0 + oc + 1],
                                            ALU.add, ALU.mult).then_inc(s_keep, 1)
                else:
                    nc.vector.scalar_tensor_tensor(keep[:, oc], gate[:, 0, oc], 1.0, C[:, 0, oc],
                                                   ALU.add, ALU.mult).then_inc(s_keep, 1)
                dve.wait_ge(s_act, n + GATES)
                nc.vector.scalar_tensor_tensor(add[:, oc], gate[:, 1, oc], 1.0, gate[:, 2, oc],
                                               ALU.add, ALU.mult).then_inc(s_add, 1)
                dve.wait_ge(s_keep, done + 1)
                dve.wait_ge(s_add, done + 1)
                if g == 1:
                    dve.wait_ge(s_clo, 2 * t + oc + 1)
                    dve.wait_ge(s_chi, 2 * t + oc + 1)
                nc.vector.scalar_tensor_tensor(C[:, t, oc], keep[:, oc], (1.0, 0.5)[t], add[:, oc],
                                               ALU.mult, ALU.add).then_inc(s_c, 1)

            def c_lo(g, t, oc):
                dve.wait_ge(s_chi, 4 * g + 2 * t + oc + 1)
                nc.vector.tensor_tensor(C_lo[:, t, oc], C[:, t, oc], C_hi[:, t, oc].bitcast(F32),
                                        ALU.subtract).then_inc(s_clo, 1)

            def output(g, j):
                dve.wait_ge(s_act, first["head", g] + j + 1)
                x1 = X[:, STEPS * g:STEPS * (g + 1), j]
                nc.vector.tensor_tensor(x1, head[:, j], x1, ALU.add).then_inc(s_y, 1)

            dve.wait_ge(s_tps, 1)
            dve.wait_ge(l_vec, 16)
            for oc in range(KC):
                nc.vector.tensor_scalar(T_T[:, oc], p_scores[:, oc * 256:oc * 256 + STEPS * KEYS],
                                        vec[:, V_ATTN + oc:V_ATTN + oc + 1], None, ALU.add).then_inc(s_tT, 1)
            stats1(0)
            dve.wait_ge(s_tmean, 1)
            for oc in range(KC):
                nc.vector.tensor_tensor(Tc_T[:, oc], T_T[:, oc], p_probsT[:, 0:STEPS * KEYS],
                                        ALU.subtract).then_inc(s_tc, 1)
            score_max(0)
            stats1(1)
            normalise(0)
            score_max(1)
            residual(0)
            normalise(1)
            layernorm(0)
            n = 2 * KC
            dve.wait_ge(s_bps, 1)
            nc.vector.tensor_tensor(bias_u[:], p_ring[3][:, 0:GATES * KC], vec[:, 0:GATES * KC], ALU.add).then_inc(s_bu, 1)
            nc.vector.tensor_scalar(bias1[:, 0:n], vec[:, 0:n], 0.5, None, ALU.mult).then_inc(s_bias, 1)
            nc.vector.tensor_copy(bias1[:, n:], vec[:, n:n + KC]).then_inc(s_bias, 1)
            dve.wait_ge(s_bu, 1)
            nc.vector.tensor_scalar(bias0[:, 0:n], bias_u[:, 0:n], 0.5, None, ALU.mult).then_inc(s_bias, 1)
            nc.vector.tensor_copy(bias0[:, n:], bias_u[:, n:]).then_inc(s_bias, 1)
            h_lo(0)
            residual(1)
            score_max_ready = 2
            stats1(2)
            layernorm(1)
            score_max(score_max_ready)
            state(0, 0, 0)
            normalise(2)
            h_lo(1)
            state(0, 0, 1)
            c_lo(0, 0, 0)
            c_lo(0, 0, 1)
            dve.wait_ge(s_bohi, 1)
            nc.vector.tensor_tensor(bo_hilo[32:33, :], bo_rows[32:33, :], bo_hilo[32:33, :].bitcast(F32),
                                    ALU.subtract).then_inc(s_bolo, 1)
            residual(2)
            stats1(3)
            layernorm(2)
            score_max(3)
            h_lo(2)
            normalise(3)
            state(0, 1, 0)
            residual(3)
            c_lo(0, 1, 0)
            state(0, 1, 1)
            c_lo(0, 1, 1)
            layernorm(3)
            state(1, 0, 0)
            h_lo(3)
            state(1, 0, 1)
            c_lo(1, 0, 0)
            c_lo(1, 0, 1)
            for j in range(TILES):
                output(0, j)
            state(1, 1, 0)
            c_lo(1, 1, 0)
            state(1, 1, 1)
            c_lo(1, 1, 1)
            for j in range(TILES):
                output(1, j)

        @block.tensor
        def _(pe):
            mm = nc.tensor.matmul

            def scores(s):
                t = s % STEPS
                pe.wait_ge(l_xT[s], 16)
                pe.wait_ge(s_tc, KC)
                if s >= 1:
                    pe.wait_ge(s_exp, TILES * s)
                for j in range(TILES):
                    for k in range(KC):
                        last = mm(p_scores[:, j * KEYS:(j + 1) * KEYS], XT[:, s % 2, k, j * P:(j + 1) * P],
                                  Tc_T[:, k, t * KEYS:(t + 1) * KEYS], start=(k == 0), stop=(k == KC - 1))
                last.then_inc(s_scores, 1)

            def probs_turn(s):
                pe.wait_ge(s_pn, s + 1)
                if s >= 1:
                    pe.wait_ge(s_pTc, s)
                for j in range(TILES):
                    last = nc.tensor.transpose(p_probsT[0:KEYS, j * P:(j + 1) * P], probs_n[:, s, j], ident[:])
                last.then_inc(s_pT, 1)

            def attend(s):
                pe.wait_ge(s_pTc, s + 1)
                if s == 0:
                    pe.wait_ge(s_trc, 1)
                if s >= 1:
                    pe.wait_ge(s_hlo, KC * s)
                for j in range(TILES):
                    a = mm(p_slab[j // 2][:, (j % 2) * D:(j % 2 + 1) * D], probs_T[:, s % 2, j * P:(j + 1) * P],
                           T_rows[:, s % STEPS], start=True, stop=True)
                    if j % 2:
                        a.then_inc(s_att, 1)

            def h_turn(s):
                pe.wait_ge(s_h, TILES * (s + 1))
                for k in range(KC):
                    for j in range(TILES):
                        last = nc.tensor.transpose(p_slab[k][:, j * P:(j + 1) * P], H[:, s % 2, j, k * P:(k + 1) * P],
                                                   ident[:])
                    last.then_inc(s_hT, 1)

            def split3(k):
                return ((0, 0), (0, 1), (1, 0))

            def gate_w(g, t, i):
                oc, q = gate_of(i)
                n = first["gates", g, t] + i
                s = STEPS * g + t
                pe.wait_ge(s_hlo, KC * (s + 1))
                if n == 0:
                    pe.wait_ge(s_wlo, KC)
                if n == 3:
                    pe.wait_ge(s_bias, 4)
                if n >= RING:
                    pe.wait_ge(s_act, n - RING + 1)
                for k in range(KC):
                    for a, b in split3(k):
                        last = mm(p_ring[n % RING][:], (W_hi, W_lo)[a][:, k, q, oc * P:(oc + 1) * P],
                                  (HT_hi, HT_lo)[b][:, s, k], start=(k == 0 and a == b),
                                  stop=(t == 0 and k == KC - 1 and a == 1))
                if t == 0:
                    last.then_inc(s_ring, 1)

            def gate_u(g, i):
                oc, q = gate_of(i)
                n = first["gates", g, 1] + i
                if g == 0 and i == 0:
                    pe.wait_ge(s_ulo, KC)
                for k in range(KC):
                    if i == 0:
                        pe.wait_ge(s_clo, 4 * g + k + 1)
                    for a, b in split3(k):
                        last = mm(p_ring[n % RING][:], (U_hi, U_lo)[a][:, k, q, oc * P:(oc + 1) * P],
                                  (C_hi, C_lo)[b][:, 0, k], start=False, stop=(k == KC - 1 and a == 1))
                last.then_inc(s_ring, 1)

            def head_w(g, j):
                n = first["head", g] + j
                if g == 0 and j == 0:
                    pe.wait_ge(s_bolo, 1)
                    pe.wait_ge(s_ones, 4)
                pe.wait_ge(s_act, n - RING + 1)
                mm(p_ring[n % RING][:], ones_r[:], bo_hilo[:], start=True, stop=False, skip_group_check=True)
                for t in range(STEPS):
                    for k in range(KC):
                        for a, b in split3(k):
                            mm(p_ring[n % RING][:, t * D:(t + 1) * D],
                               (HT_hi, HT_lo)[a][:, STEPS * g + t, k, j * P:(j + 1) * P],
                               (W_hi, W_lo)[b][:, k, HEAD], start=False, stop=False, skip_group_check=True)

            def head_c(g, j):
                n = first["head", g] + j
                for k in range(KC):
                    if j == 0:
                        pe.wait_ge(s_clo, 4 * g + 2 + k + 1)
                    for a, b in split3(k):
                        u = (U_hi, U_lo)[b][:, k, HEAD].unsqueeze(1).to_broadcast([P, STEPS, D])
                        last = mm(p_ring[n % RING][:].rearrange("p (t d) -> p t d", t=STEPS),
                                  (C_hi, C_lo)[a][:, 1, k, j * P:(j + 1) * P], u, start=False,
                                  stop=(k == KC - 1 and a == 1), skip_group_check=True)
                last.then_inc(s_ring, 1)

            pe.wait_ge(l_cw, 16)
            for oc in range(KC):
                for k in range(KC):
                    last = mm(p_scores[:, oc * 256:oc * 256 + STEPS * KEYS], CW[:, k, oc * P:(oc + 1) * P],
                              CW[:, k, D:D + STEPS * KEYS], start=(k == 0), stop=(k == KC - 1))
            last.then_inc(s_tps, 1)
            pe.wait_ge(s_ones, 1)
            pe.wait_ge(s_tT, KC)
            for oc in range(KC):
                last = mm(p_probsT[:, 0:STEPS * KEYS], mean_w[:], T_T[:, oc], start=(oc == 0), stop=(oc == KC - 1))
            last.then_inc(s_tmean, 1)
            pe.wait_ge(s_ident, 1)
            for t in range(STEPS):
                for oc in range(KC):
                    last = nc.tensor.transpose(p_slab[0][0:KEYS, t * D + oc * P:t * D + (oc + 1) * P],
                                               T_T[:, oc, t * KEYS:(t + 1) * KEYS], ident[:])
            last.then_inc(s_trows, 1)

            scores(0)
            probs_turn(0)
            scores(1)
            attend(0)
            pe.wait_ge(l_u, 16)
            pe.wait_ge(l_vec, 16)
            for q in range(GATES):
                for oc in range(KC):
                    c = q * KC + oc
                    for k in range(KC):
                        last = mm(p_ring[3][:, c:c + 1], U[:, k, q, oc * P:(oc + 1) * P],
                                  vec[:, V_C0 + k:V_C0 + k + 1], start=(k == 0), stop=(k == KC - 1))
            last.then_inc(s_bps, 1)
            probs_turn(1)
            h_turn(0)
            gate_w(0, 0, 0)
            attend(1)
            gate_w(0, 0, 1)
            scores(2)
            gate_w(0, 0, 2)
            gate_w(0, 0, 3)
            h_turn(1)
            gate_w(0, 0, 4)
            probs_turn(2)
            gate_w(0, 0, 5)
            for i in range(2):
                gate_w(0, 1, i)
            attend(2)
            for i in range(2, 4):
                gate_w(0, 1, i)
            gate_u(0, 0)
            scores(3)
            gate_u(0, 1)
            gate_w(0, 1, 4)
            h_turn(2)
            gate_u(0, 2)
            gate_w(0, 1, 5)
            probs_turn(3)
            gate_u(0, 3)
            attend(3)
            gate_u(0, 4)
            gate_u(0, 5)
            for i in range(3):
                gate_w(1, 0, i)
            h_turn(3)
            for i in range(3, 6):
                gate_w(1, 0, i)
            for g in range(GROUPS):
                if g == 1:
                    for i in range(4):
                        gate_w(1, 1, i)
                    gate_u(1, 0)
                    gate_u(1, 1)
                    gate_w(1, 1, 4)
                    gate_u(1, 2)
                    gate_w(1, 1, 5)
                    for i in range(3, 6):
                        gate_u(1, i)
                head_w(g, 0)
                head_w(g, 1)
                head_c(g, 0)
                head_w(g, 2)
                head_c(g, 1)
                head_w(g, 3)
                head_c(g, 2)
                head_c(g, 3)


def kernel(**inputs):
    import numpy as np
    import concourse.bacc as bacc
    from concourse.bass_utils import run_bass_kernel_spmd

    def rows(name):
        return np.asarray(inputs[name])

    def chunks(a):
        return a.reshape(KC, P, -1).transpose(1, 0, 2)

    x = rows("x")
    xT = x.reshape(STEPS, GROUPS, P, TILES, KC, P).transpose(5, 1, 0, 4, 3, 2).reshape(P, SLABS, KC, SLAB)
    ctx_w = np.concatenate([chunks(rows("L0_xattn_W").T), chunks(rows("ctx_1024").reshape(-1, D).T)], axis=2)
    wT = np.stack([chunks(rows("L0_ffn_" + n).T) for n in ("wf", "wi", "wc", "wo")], axis=2)
    uT = np.stack([chunks(rows("L0_ffn_" + n).T) for n in ("uf", "ui", "uc", "uo")], axis=2)
    vecs = np.concatenate([rows(n).reshape(KC, P).T for n in
                           ("L0_ffn_bf", "L0_ffn_bi", "L0_ffn_bc", "L0_xattn_b", "L0_ffn_in_c")], axis=1)
    arrays = {"x": x, "xT": xT, "ctx_w": ctx_w, "wT": wT, "uT": uT, "vecs": vecs,
              "bo": rows("L0_ffn_bo").reshape(1, D)}
    arrays = {n: np.ascontiguousarray(a) for n, a in arrays.items()}

    nc = bacc.Bacc("TRN2", target_bir_lowering=False, num_devices=1)
    aps = {n: nc.dram_tensor(n, a.shape, F32, kind="ExternalInput").ap() for n, a in arrays.items()}
    out = nc.dram_tensor("out", x.shape, F32, kind="ExternalOutput").ap()
    build(nc, out=out, **aps)
    r = run_bass_kernel_spmd(nc, [arrays], core_ids=[0])
    return r.results[0]["out"]
```

```python
from contextlib import ExitStack

import concourse.bass as bass
from concourse import mybir

F32 = mybir.dt.float32
F32R = mybir.dt.float32r
ALU = mybir.AluOpType
ACT = mybir.ActivationFunctionType
AX = mybir.AxisListType

P = 128
STEPS, ROWS, D = 2, 1024, 256
KEYS = 77
KC = D // P
GROUPS = 2
SLAB = ROWS // GROUPS
TILES = SLAB // P
SLABS = GROUPS * STEPS
EPS = 1e-5
GATES = 3
HEAD = 3
RING = 4
V_GATE, V_ATTN, V_C0, V_COUNT = 0, GATES * KC, GATES * KC + KC, GATES * KC + 2 * KC


def build(nc, x, xT, ctx_w, wT, uT, vecs, bo, out):
    with ExitStack() as ctx:
        def sb(name, shape, dt=F32):
            return ctx.enter_context(nc.sbuf_tensor(name, shape, dt))

        def psum(name):
            return ctx.enter_context(nc.psum_tensor(name, [P, 512], F32))

        def sem(name):
            return ctx.enter_context(nc.semaphore(name))

        X = sb("X", [P, SLABS, TILES, D])
        XT = sb("XT", [P, 2, KC, SLAB])
        CW = sb("CW", [P, KC, D + STEPS * KEYS])
        W = sb("W", [P, KC, HEAD + 1, D])
        U = sb("U", [P, KC, HEAD + 1, D])
        W_hi = sb("W_hi", [P, KC, HEAD + 1, D], F32R)
        W_lo = sb("W_lo", [P, KC, HEAD + 1, D], F32R)
        U_hi = sb("U_hi", [P, KC, HEAD + 1, D], F32R)
        U_lo = sb("U_lo", [P, KC, HEAD + 1, D], F32R)
        vec = sb("vec", [P, V_COUNT])
        bo_all = sb("bo_all", [P, D])
        ident = sb("ident", [P, P])
        mean_w = sb("mean_w", [P, P])
        neg_half = sb("neg_half", [P, TILES])
        T_T = sb("T_T", [P, KC, STEPS * KEYS])
        Tc_T = sb("Tc_T", [P, KC, STEPS * KEYS])
        T_rows = sb("T_rows", [KEYS, STEPS, D])
        bias0 = sb("bias0", [P, GATES * KC])
        bias1 = sb("bias1", [P, GATES * KC])
        bias_u = sb("bias_u", [P, GATES * KC])
        st1 = sb("st1", [P, SLABS, TILES, 6])
        mv1 = sb("mv1", [P, SLABS, TILES, 2])
        ve1 = sb("ve1", [P, SLABS, TILES])
        rstd1 = sb("rstd1", [P, SLABS, TILES])
        st2 = sb("st2", [P, SLABS, TILES, 6])
        mv2 = sb("mv2", [P, SLABS, TILES, 2])
        ve2 = sb("ve2", [P, SLABS, TILES])
        rstd2 = sb("rstd2", [P, SLABS, TILES])
        row_max = sb("row_max", [P, SLABS, TILES])
        exp_bias = sb("exp_bias", [P, SLABS, TILES])
        row_sum = sb("row_sum", [P, SLABS, TILES])
        row_rec = sb("row_rec", [P, SLABS, TILES])
        probs = sb("probs", [P, SLABS, TILES, KEYS])
        probs_n = sb("probs_n", [P, SLABS, TILES, KEYS])
        probs_T = sb("probs_T", [KEYS, 2, SLAB])
        H = sb("H", [P, 2, TILES, D])
        HT_hi = sb("HT_hi", [P, SLABS, KC, SLAB], F32R)
        HT_lo = sb("HT_lo", [P, SLABS, KC, SLAB], F32R)
        gate = sb("gate", [P, GATES, KC, SLAB])
        keep = sb("keep", [P, KC, SLAB])
        add = sb("add", [P, KC, SLAB])
        C = sb("C", [P, 2, KC, SLAB])
        C_hi = sb("C_hi", [P, 2, KC, SLAB], F32R)
        C_lo = sb("C_lo", [P, 2, KC, SLAB], F32R)
        head_c = sb("head_c", [P, TILES, D])
        head = sb("head", [P, TILES, STEPS, D])
        warm = sb("warm", [P, 1])
        idle = sb("idle", [P, P], mybir.dt.bfloat16)

        p_scores = psum("p_scores")
        p_probsT = psum("p_probsT")
        p_slab = [psum(f"p_slab{k}") for k in range(2)]
        p_ring = [psum(f"p_ring{k}") for k in range(RING)]
        p_head_c = [p_scores, p_probsT, *p_slab]

        def p_att(s):
            return p_ring[2:4] if s == 1 else p_slab

        l_cw, l_vec, l_bo, l_w, l_u = (sem(n) for n in ("l_cw", "l_vec", "l_bo", "l_w", "l_u"))
        l_x = [sem(f"l_x{s}") for s in range(SLABS)]
        l_xT = [sem(f"l_xT{s}") for s in range(SLABS)]
        stored = [sem(f"stored{j}") for j in range(TILES)]
        s_warm = sem("s_warm")
        s_zero = sem("s_zero")
        s_ident = sem("s_ident")
        s_idle = sem("s_idle")
        s_half = sem("s_half")
        s_mean = sem("s_mean")
        s_whi = sem("s_whi")
        s_wlo0 = sem("s_wlo0")
        s_wlo1 = sem("s_wlo1")
        s_uhi = sem("s_uhi")
        s_ulo = sem("s_ulo")
        s_tps = sem("s_tps")
        s_tT = sem("s_tT")
        s_tmean = sem("s_tmean")
        s_trows = sem("s_trows")
        s_tc = sem("s_tc")
        s_trc = sem("s_trc")
        s_bps = sem("s_bps")
        s_bu = sem("s_bu")
        s_bias = sem("s_bias")
        s_st1, s_mv1, s_ve1, s_rstd1 = (sem(n) for n in ("s_st1", "s_mv1", "s_ve1", "s_rstd1"))
        s_scores = sem("s_scores")
        s_max = sem("s_max")
        s_ebias = sem("s_ebias")
        s_exp = sem("s_exp")
        s_rec = sem("s_rec")
        s_pn = sem("s_pn")
        s_pT = sem("s_pT")
        s_pTc = sem("s_pTc")
        s_att = sem("s_att")
        s_x1 = sem("s_x1")
        s_st2, s_mv2, s_ve2, s_rstd2 = (sem(n) for n in ("s_st2", "s_mv2", "s_ve2", "s_rstd2"))
        s_h = sem("s_h")
        s_hT = sem("s_hT")
        s_hhi = sem("s_hhi")
        s_hlo = sem("s_hlo")
        s_ring = sem("s_ring")
        s_act = sem("s_act")
        s_keep = sem("s_keep")
        s_add = sem("s_add")
        s_c = sem("s_c")
        s_chi = sem("s_chi")
        s_clo = sem("s_clo")
        s_hc = sem("s_hc")
        s_hcb = sem("s_hcb")
        s_pre = sem("s_pre")
        s_tanh = sem("s_tanh")
        s_y = sem("s_y")

        first = {("gates", 0, 0): 0, ("gates", 0, 1): 6, ("gates", 1, 0): 12, ("head", 0): 18,
                 ("gates", 1, 1): 22, ("head", 1): 28}

        def taken(n):
            return n + 1 - TILES * sum(first["head", g] < n for g in range(GROUPS))

        def gate_of(i):
            return i // GATES, i % GATES

        block = ctx.enter_context(nc.Block())

        @block.sync
        def _(sp):
            sp.dma_start(CW[:], ctx_w).then_inc(l_cw, 16)
            sp.dma_start(vec[:], vecs).then_inc(l_vec, 16)

            def load_slab(s):
                if s >= 2:
                    sp.wait_ge(s_scores, s - 1)
                sp.dma_start(XT[:, s % 2], xT[:, s]).then_inc(l_xT[s], 16)
                g, t = s // STEPS, s % STEPS
                rows = x[t, g * SLAB:(g + 1) * SLAB, :].rearrange("(p j) d -> p j d", j=TILES)
                sp.dma_start(X[:, s], rows).then_inc(l_x[s], 16)

            load_slab(0)
            sp.dma_start(U[:], uT).then_inc(l_u, 16)
            load_slab(1)
            sp.dma_start(W[:], wT).then_inc(l_w, 16)
            load_slab(2)
            sp.dma_start(bo_all[:], bo.to_broadcast([P, D])).then_inc(l_bo, 16)
            load_slab(3)
            for g in range(GROUPS):
                for j in range(TILES):
                    sp.wait_ge(s_y, g * TILES + j + 1)
                    rows = out[:, g * SLAB:(g + 1) * SLAB, :].rearrange("t (p j) d -> p j t d", j=TILES)
                    sp.dma_start(rows[:, j], X[:, STEPS * g:STEPS * (g + 1), j]).then_inc(stored[j], 16)
            for j in range(TILES):
                sp.wait_ge(stored[j], 16 * GROUPS)

        @block.gpsimd
        def _(pool):
            nc.gpsimd.memset(ident[:], 0.0).then_inc(s_zero, 1)
            pool.wait_ge(s_zero, 1)
            nc.gpsimd.affine_select(out=ident[:], in_=ident[:], compare_op=ALU.not_equal, fill=1.0, base=0,
                                    pattern=[[-1, P]], channel_multiplier=1).then_inc(s_ident, 1)
            nc.gpsimd.memset(neg_half[:], -0.5).then_inc(s_half, 1)
            pool.wait_ge(s_half, 1)

            def deviation1(s):
                pool.wait_ge(s_mv1, TILES * (s + 1))
                nc.gpsimd.tensor_scalar(ve1[:, s], mv1[:, s, :, 1], EPS, 1.0, ALU.add, ALU.mult).then_inc(s_ve1, 1)
                pool.wait_ge(s_ve1, s + 1)
                nc.gpsimd.tensor_tensor(rstd1[:, s], ve1[:, s], neg_half[:], ALU.pow).then_inc(s_rstd1, 1)

            def deviation2(s):
                pool.wait_ge(s_mv2, TILES * (s + 1))
                nc.gpsimd.tensor_scalar(ve2[:, s], mv2[:, s, :, 1], EPS, 1.0, ALU.add, ALU.mult).then_inc(s_ve2, 1)
                pool.wait_ge(s_ve2, s + 1)
                nc.gpsimd.tensor_tensor(rstd2[:, s], ve2[:, s], neg_half[:], ALU.pow).then_inc(s_rstd2, 1)

            def u_lo(k):
                pool.wait_ge(s_uhi, k + 1)
                nc.gpsimd.tensor_tensor(U_lo[:, k], U[:, k], U_hi[:, k].bitcast(F32), ALU.subtract).then_inc(s_ulo, 1)

            deviation1(0)
            deviation1(1)
            pool.wait_ge(s_whi, KC)
            deviation2(0)
            nc.gpsimd.tensor_tensor(W_lo[:, 1], W[:, 1], W_hi[:, 1].bitcast(F32), ALU.subtract).then_inc(s_wlo1, 1)
            deviation1(2)
            u_lo(0)
            deviation2(1)
            u_lo(1)
            deviation1(3)
            deviation2(2)
            deviation2(3)

        @block.scalar
        def _(act):
            act.wait_ge(s_warm, 1)
            nc.scalar.activation(warm[:], warm[:], ACT.Exp).then_inc(s_warm, 1)

            def exponentials(s):
                act.wait_ge(s_ebias, s + 1)
                for j in range(TILES):
                    e = nc.scalar.activation(probs[:, s, j], p_scores[:, j * KEYS:(j + 1) * KEYS], ACT.Exp,
                                             bias=exp_bias[:, s, j:j + 1], scale=rstd1[:, s, j:j + 1],
                                             accum_out=row_sum[:, s, j:j + 1])
                    e.then_inc(s_exp, 1)

            def probs_T_copy(s):
                act.wait_ge(s_pT, s + 1)
                if s >= 2:
                    act.wait_ge(s_att, 2 * (s - 1))
                nc.scalar.copy(probs_T[:, s % 2], p_probsT[0:KEYS, :]).then_inc(s_pTc, 1)

            def h_hi(s):
                for k in range(KC):
                    act.wait_ge(s_hT, KC * s + k + 1)
                    nc.scalar.copy(HT_hi[:, s, k], p_slab[k][:]).then_inc(s_hhi, 1)

            def gate_tanh(g, t, i):
                n = first["gates", g, t] + i
                oc, q = gate_of(i)
                act.wait_ge(s_ring, n + 1)
                if (t, i) == (0, 0):
                    act.wait_ge(s_bias, 4)
                if (g, t) != (0, 0):
                    act.wait_ge(s_keep, 4 * g + 2 * t + oc - 1)
                    act.wait_ge(s_add, 4 * g + 2 * t + oc - 1)
                bias = (bias0, bias1)[t]
                c = q * KC + oc
                nc.scalar.activation(gate[:, q, oc], p_ring[n % RING][:], ACT.Tanh, bias=bias[:, c:c + 1],
                                     scale=1.0 if q == 2 else 0.5).then_inc(s_act, 1)

            def c_hi(g, t, oc):
                act.wait_ge(s_c, 4 * g + 2 * t + oc + 1)
                if g == 1 and t == 0:
                    act.wait_ge(s_ring, 12)
                if g == 1 and t == 1:
                    act.wait_ge(s_hc, TILES)
                nc.scalar.mul(C_hi[:, t, oc], C[:, t, oc], 0.5).then_inc(s_chi, 1)

            def head_tanh(g, j):
                act.wait_ge(s_pre, TILES * g + j + 1)
                nc.scalar.activation(head[:, j], head[:, j], ACT.Tanh).then_inc(s_tanh, 1)

            def w_hi(k):
                act.wait_ge(l_w, 16)
                nc.scalar.copy(W_hi[:, k], W[:, k]).then_inc(s_whi, 1)

            def u_hi(k):
                act.wait_ge(l_u, 16)
                nc.scalar.copy(U_hi[:, k], U[:, k]).then_inc(s_uhi, 1)

            act.wait_ge(s_trows, 1)
            nc.scalar.copy(T_rows[:], p_slab[0][0:KEYS, :].rearrange("p (t d) -> p t d", t=STEPS)).then_inc(s_trc, 1)
            exponentials(0)
            u_hi(0)
            probs_T_copy(0)
            u_hi(1)
            w_hi(0)
            w_hi(1)
            exponentials(1)
            h_hi(0)
            probs_T_copy(1)
            gate_tanh(0, 0, 0)
            gate_tanh(0, 0, 1)
            exponentials(2)
            gate_tanh(0, 0, 2)
            h_hi(1)
            gate_tanh(0, 0, 3)
            probs_T_copy(2)
            c_hi(0, 0, 0)
            gate_tanh(0, 0, 4)
            gate_tanh(0, 0, 5)
            c_hi(0, 0, 1)
            gate_tanh(0, 1, 0)
            exponentials(3)
            gate_tanh(0, 1, 1)
            h_hi(2)
            gate_tanh(0, 1, 2)
            probs_T_copy(3)
            gate_tanh(0, 1, 3)
            c_hi(0, 1, 0)
            gate_tanh(0, 1, 4)
            gate_tanh(0, 1, 5)
            c_hi(0, 1, 1)
            for i in range(3):
                gate_tanh(1, 0, i)
            h_hi(3)
            for i in range(3, 5):
                gate_tanh(1, 0, i)
            c_hi(1, 0, 0)
            gate_tanh(1, 0, 5)
            c_hi(1, 0, 1)
            for j in range(TILES):
                head_tanh(0, j)
            for i in range(5):
                gate_tanh(1, 1, i)
            c_hi(1, 1, 0)
            gate_tanh(1, 1, 5)
            c_hi(1, 1, 1)
            for j in range(TILES):
                head_tanh(1, j)

        @block.vector
        def _(dve):
            nc.vector.memset(idle[:], 0.0).then_inc(s_idle, 1)
            nc.vector.memset(warm[:], 0.0).then_inc(s_warm, 1)
            nc.vector.memset(mean_w[:], 1.0 / D).then_inc(s_mean, 1)

            def centre_t():
                dve.wait_ge(s_tmean, 1)
                for oc in range(KC):
                    nc.vector.tensor_tensor(Tc_T[:, oc], T_T[:, oc], p_probsT[:, 0:STEPS * KEYS],
                                            ALU.subtract).then_inc(s_tc, 1)

            def stats1(s):
                dve.wait_ge(l_x[s], 16)
                for j in range(TILES):
                    if (s, j) == (0, TILES - 1):
                        centre_t()
                    nc.vector.bn_stats(st1[:, s, j], X[:, s, j]).then_inc(s_st1, 1)
                for j in range(TILES):
                    dve.wait_ge(s_st1, TILES * s + j + 1)
                    nc.vector.bn_aggr(mv1[:, s, j], st1[:, s, j]).then_inc(s_mv1, 1)

            def score_max(s):
                dve.wait_ge(s_scores, s + 1)
                nc.vector.tensor_reduce(row_max[:, s], p_scores[:, 0:TILES * KEYS].rearrange("p (j k) -> p j k", j=TILES),
                                        AX.X, ALU.max).then_inc(s_max, 1)
                dve.wait_ge(s_max, s + 1)
                dve.wait_ge(s_rstd1, s + 1)
                nc.vector.scalar_tensor_tensor(exp_bias[:, s], row_max[:, s], -1.0, rstd1[:, s], ALU.mult,
                                               ALU.mult).then_inc(s_ebias, 1)

            def normalise(s):
                dve.wait_ge(s_exp, TILES * (s + 1))
                nc.vector.reciprocal(row_rec[:, s], row_sum[:, s]).then_inc(s_rec, 1)
                dve.wait_ge(s_rec, s + 1)
                rec = row_rec[:, s].unsqueeze(2).to_broadcast([P, TILES, KEYS])
                nc.vector.tensor_tensor(probs_n[:, s], probs[:, s], rec, ALU.mult).then_inc(s_pn, 1)

            def residual(s):
                for i in range(2):
                    dve.wait_ge(s_att, 2 * s + i + 1)
                    nc.vector.scalar_tensor_tensor(X[:, s, 2 * i:2 * i + 2],
                                                   p_att(s)[i][:].rearrange("p (j d) -> p j d", j=2), 0.0,
                                                   X[:, s, 2 * i:2 * i + 2], ALU.max, ALU.add).then_inc(s_x1, 1)
                    dve.wait_ge(s_x1, 2 * s + i + 1)
                    for j in (2 * i, 2 * i + 1):
                        nc.vector.bn_stats(st2[:, s, j], X[:, s, j]).then_inc(s_st2, 1)
                for j in range(TILES):
                    dve.wait_ge(s_st2, TILES * s + j + 1)
                    nc.vector.bn_aggr(mv2[:, s, j], st2[:, s, j]).then_inc(s_mv2, 1)

            def layernorm(s):
                dve.wait_ge(s_rstd2, s + 1)
                if s >= 2:
                    dve.wait_ge(s_hT, KC * (s - 1))
                for j in range(TILES):
                    nc.vector.tensor_scalar(H[:, s % 2, j], X[:, s, j], mv2[:, s, j, 0:1], rstd2[:, s, j:j + 1],
                                            ALU.subtract, ALU.mult).then_inc(s_h, 1)

            def h_lo(s):
                for k in range(KC):
                    dve.wait_ge(s_hhi, KC * s + k + 1)
                    nc.vector.tensor_tensor(HT_lo[:, s, k], p_slab[k][:], HT_hi[:, s, k].bitcast(F32),
                                            ALU.subtract).then_inc(s_hlo, 1)

            def state(g, t, oc):
                n = first["gates", g, t] + GATES * oc
                done = 4 * g + 2 * t + oc
                dve.wait_ge(s_act, taken(n))
                if done >= 2:
                    dve.wait_ge(s_c, done - 1)
                if t == 0:
                    nc.vector.tensor_scalar(keep[:, oc], gate[:, 0, oc], 1.0, vec[:, V_C0 + oc:V_C0 + oc + 1],
                                            ALU.add, ALU.mult).then_inc(s_keep, 1)
                else:
                    nc.vector.scalar_tensor_tensor(keep[:, oc], gate[:, 0, oc], 1.0, C[:, 0, oc],
                                                   ALU.add, ALU.mult).then_inc(s_keep, 1)
                dve.wait_ge(s_act, taken(n + GATES - 1))
                nc.vector.scalar_tensor_tensor(add[:, oc], gate[:, 1, oc], 1.0, gate[:, 2, oc],
                                               ALU.add, ALU.mult).then_inc(s_add, 1)
                dve.wait_ge(s_keep, done + 1)
                dve.wait_ge(s_add, done + 1)
                if g == 1:
                    dve.wait_ge(s_clo, 2 * t + oc + 1)
                nc.vector.scalar_tensor_tensor(C[:, t, oc], keep[:, oc], (1.0, 0.5)[t], add[:, oc],
                                               ALU.mult, ALU.add).then_inc(s_c, 1)

            def c_lo(g, t, oc):
                dve.wait_ge(s_chi, 4 * g + 2 * t + oc + 1)
                nc.vector.scalar_tensor_tensor(C_lo[:, t, oc], C[:, t, oc], 0.5, C_hi[:, t, oc].bitcast(F32),
                                               ALU.mult, ALU.subtract).then_inc(s_clo, 1)

            def head_bias(g, j):
                if (g, j) == (0, 0):
                    dve.wait_ge(l_bo, 16)
                dve.wait_ge(s_hc, TILES * g + j + 1)
                if g == 1:
                    dve.wait_ge(s_pre, j + 1)
                nc.vector.tensor_tensor(head_c[:, j], p_head_c[j][:, 0:D], bo_all[:], ALU.add).then_inc(s_hcb, 1)

            def head_sum(g, j):
                n = first["head", g] + j
                dve.wait_ge(s_ring, n + 1)
                dve.wait_ge(s_hcb, TILES * g + j + 1)
                if g == 1:
                    dve.wait_ge(s_y, j + 1)
                c = head_c[:, j].unsqueeze(1).to_broadcast([P, STEPS, D])
                nc.vector.tensor_tensor(head[:, j], p_ring[n % RING][:].rearrange("p (t d) -> p t d", t=STEPS), c,
                                        ALU.add).then_inc(s_pre, 1)

            def output(g, j):
                dve.wait_ge(s_tanh, TILES * g + j + 1)
                x1 = X[:, STEPS * g:STEPS * (g + 1), j]
                nc.vector.tensor_tensor(x1, head[:, j], x1, ALU.add).then_inc(s_y, 1)

            dve.wait_ge(s_tps, 1)
            dve.wait_ge(l_vec, 16)
            for oc in range(KC):
                nc.vector.tensor_scalar(T_T[:, oc], p_scores[:, oc * 256:oc * 256 + STEPS * KEYS],
                                        vec[:, V_ATTN + oc:V_ATTN + oc + 1], None, ALU.add).then_inc(s_tT, 1)
            stats1(0)
            score_max(0)
            normalise(0)
            stats1(1)
            residual(0)
            score_max(1)
            layernorm(0)
            normalise(1)
            n = 2 * KC
            nc.vector.tensor_scalar(bias1[:, 0:n], vec[:, 0:n], 0.5, None, ALU.mult).then_inc(s_bias, 1)
            nc.vector.tensor_copy(bias1[:, n:], vec[:, n:n + KC]).then_inc(s_bias, 1)
            dve.wait_ge(s_bps, KC)
            nc.vector.tensor_tensor(bias_u[:], p_ring[1][:, 0:GATES * KC], vec[:, 0:GATES * KC], ALU.add).then_inc(s_bu, 1)
            dve.wait_ge(s_bu, 1)
            nc.vector.tensor_scalar(bias0[:, 0:n], bias_u[:, 0:n], 0.5, None, ALU.mult).then_inc(s_bias, 1)
            nc.vector.tensor_copy(bias0[:, n:], bias_u[:, n:]).then_inc(s_bias, 1)
            dve.wait_ge(s_whi, 1)
            nc.vector.tensor_tensor(W_lo[:, 0], W[:, 0], W_hi[:, 0].bitcast(F32), ALU.subtract).then_inc(s_wlo0, 1)
            h_lo(0)
            stats1(2)
            residual(1)
            score_max(2)
            layernorm(1)
            normalise(2)
            stats1(3)
            h_lo(1)
            state(0, 0, 0)
            c_lo(0, 0, 0)
            residual(2)
            state(0, 0, 1)
            c_lo(0, 0, 1)
            layernorm(2)
            score_max(3)
            h_lo(2)
            normalise(3)
            state(0, 1, 0)
            residual(3)
            c_lo(0, 1, 0)
            state(0, 1, 1)
            c_lo(0, 1, 1)
            layernorm(3)
            state(1, 0, 0)
            h_lo(3)
            c_lo(1, 0, 0)
            state(1, 0, 1)
            c_lo(1, 0, 1)
            for g in range(GROUPS):
                if g == 1:
                    for oc in range(KC):
                        state(1, 1, oc)
                        c_lo(1, 1, oc)
                head_bias(g, 0)
                head_sum(g, 0)
                for j in range(1, TILES):
                    head_bias(g, j)
                    head_sum(g, j)
                    output(g, j - 1)
                output(g, TILES - 1)

        @block.tensor
        def _(pe):
            mm = nc.tensor.matmul

            def scores(s):
                t = s % STEPS
                pe.wait_ge(l_xT[s], 16)
                pe.wait_ge(s_tc, KC)
                if s >= 1:
                    pe.wait_ge(s_exp, TILES * s)
                for j in range(TILES):
                    for k in range(KC):
                        last = mm(p_scores[:, j * KEYS:(j + 1) * KEYS], XT[:, s % 2, k, j * P:(j + 1) * P],
                                  Tc_T[:, k, t * KEYS:(t + 1) * KEYS], start=(k == 0), stop=(k == KC - 1))
                last.then_inc(s_scores, 1)

            def probs_turn(s):
                pe.wait_ge(s_pn, s + 1)
                if s >= 1:
                    pe.wait_ge(s_pTc, s)
                for j in range(TILES):
                    last = nc.tensor.transpose(p_probsT[0:KEYS, j * P:(j + 1) * P], probs_n[:, s, j], ident[:])
                last.then_inc(s_pT, 1)

            def attend(s):
                pe.wait_ge(s_pTc, s + 1)
                if s == 0:
                    pe.wait_ge(s_trc, 1)
                if s >= 2:
                    pe.wait_ge(s_hlo, KC * s)
                for j in range(TILES):
                    a = mm(p_att(s)[j // 2][:, (j % 2) * D:(j % 2 + 1) * D], probs_T[:, s % 2, j * P:(j + 1) * P],
                           T_rows[:, s % STEPS], start=True, stop=True)
                    if j % 2:
                        a.then_inc(s_att, 1)

            def h_turn(s):
                pe.wait_ge(s_h, TILES * (s + 1))
                if s == 1:
                    pe.wait_ge(s_hlo, KC)
                for k in range(KC):
                    for j in range(TILES):
                        last = nc.tensor.transpose(p_slab[k][:, j * P:(j + 1) * P], H[:, s % 2, j, k * P:(k + 1) * P],
                                                   ident[:])
                    last.then_inc(s_hT, 1)

            def split3(k):
                return ((0, 0), (0, 1), (1, 0))

            def wait_bank(n):
                for g in range(GROUPS):
                    if 0 <= n - RING - first["head", g] < TILES:
                        pe.wait_ge(s_pre, TILES * g + n - RING - first["head", g] + 1)
                        return
                if n >= RING:
                    pe.wait_ge(s_act, taken(n - RING))

            def gate_w(g, t, i):
                oc, q = gate_of(i)
                n = first["gates", g, t] + i
                s = STEPS * g + t
                pe.wait_ge(s_hlo, KC * (s + 1))
                if n == 0:
                    pe.wait_ge(s_wlo0, 1)
                    pe.wait_ge(s_wlo1, 1)
                if n == 1:
                    pe.wait_ge(s_bu, 1)
                if n in (2, 3):
                    pe.wait_ge(s_x1, 4)
                wait_bank(n)
                for k in range(KC):
                    for a, b in split3(k):
                        last = mm(p_ring[n % RING][:], (W_hi, W_lo)[a][:, k, q, oc * P:(oc + 1) * P],
                                  (HT_hi, HT_lo)[b][:, s, k], start=(k == 0 and a == b),
                                  stop=(t == 0 and k == KC - 1 and a == 1))
                if t == 0:
                    last.then_inc(s_ring, 1)

            def gate_u(g, i):
                oc, q = gate_of(i)
                n = first["gates", g, 1] + i
                if g == 0 and i == 0:
                    pe.wait_ge(s_ulo, KC)
                for k in range(KC):
                    if i == 0:
                        pe.wait_ge(s_clo, 4 * g + k + 1)
                    for a, b in split3(k):
                        last = mm(p_ring[n % RING][:], (U_hi, U_lo)[a][:, k, q, oc * P:(oc + 1) * P],
                                  (C_hi, C_lo)[b][:, 0, k], start=False, stop=(k == KC - 1 and a == 1))
                last.then_inc(s_ring, 1)

            def head_w(g, j):
                n = first["head", g] + j
                wait_bank(n)
                for t in range(STEPS):
                    for k in range(KC):
                        for a, b in split3(k):
                            last = mm(p_ring[n % RING][:, t * D:(t + 1) * D],
                                      (HT_hi, HT_lo)[a][:, STEPS * g + t, k, j * P:(j + 1) * P],
                                      (W_hi, W_lo)[b][:, k, HEAD], start=(k == 0 and a == b),
                                      stop=(k == KC - 1 and a == 1))
                last.then_inc(s_ring, 1)

            def head_c_part(g, j):
                if g == 0:
                    pe.wait_ge(*((s_exp, TILES * SLABS), (s_pTc, SLABS), (s_hlo, KC * SLABS), (s_hlo, KC * SLABS))[j])
                else:
                    pe.wait_ge(s_hcb, j + 1)
                for k in range(KC):
                    if j == 0:
                        pe.wait_ge(s_clo, 4 * g + 2 + k + 1)
                    for a, b in split3(k):
                        last = mm(p_head_c[j][:, 0:D], (C_hi, C_lo)[a][:, 1, k, j * P:(j + 1) * P],
                                  (U_hi, U_lo)[b][:, k, HEAD], start=(k == 0 and a == b),
                                  stop=(k == KC - 1 and a == 1))
                last.then_inc(s_hc, 1)

            def keep_warm(n):
                for _ in range(n):
                    mm(p_ring[0][:, 0:P], idle[:], idle[:], start=True, stop=True)

            def u_c0(oc):
                pe.wait_ge(l_u, 16)
                pe.wait_ge(l_vec, 16)
                for q in range(GATES):
                    c = q * KC + oc
                    for k in range(KC):
                        last = mm(p_ring[1][:, c:c + 1], U[:, k, q, oc * P:(oc + 1) * P],
                                  vec[:, V_C0 + k:V_C0 + k + 1], start=(k == 0), stop=(k == KC - 1))
                        keep_warm(2)
                last.then_inc(s_bps, 1)

            pe.wait_ge(s_idle, 1)
            keep_warm(32)
            pe.wait_ge(l_cw, 16)
            for oc in range(KC):
                for k in range(KC):
                    last = mm(p_scores[:, oc * 256:oc * 256 + STEPS * KEYS], CW[:, k, oc * P:(oc + 1) * P],
                              CW[:, k, D:D + STEPS * KEYS], start=(k == 0), stop=(k == KC - 1))
            last.then_inc(s_tps, 1)
            pe.wait_ge(s_tT, KC)
            pe.wait_ge(s_mean, 1)
            for oc in range(KC):
                last = mm(p_probsT[:, 0:STEPS * KEYS], mean_w[:], T_T[:, oc], start=(oc == 0), stop=(oc == KC - 1))
            last.then_inc(s_tmean, 1)
            pe.wait_ge(s_ident, 1)
            for t in range(STEPS):
                for oc in range(KC):
                    last = nc.tensor.transpose(p_slab[0][0:KEYS, t * D + oc * P:t * D + (oc + 1) * P],
                                               T_T[:, oc, t * KEYS:(t + 1) * KEYS], ident[:])
            last.then_inc(s_trows, 1)

            keep_warm(10)
            scores(0)
            u_c0(0)
            keep_warm(20)
            probs_turn(0)
            keep_warm(8)
            attend(0)
            scores(1)
            u_c0(1)
            keep_warm(30)
            h_turn(0)
            probs_turn(1)
            keep_warm(12)
            gate_w(0, 0, 0)
            attend(1)
            gate_w(0, 0, 1)
            scores(2)
            gate_w(0, 0, 2)
            gate_w(0, 0, 3)
            h_turn(1)
            probs_turn(2)
            gate_w(0, 0, 4)
            attend(2)
            gate_w(0, 0, 5)
            for i in range(4):
                gate_w(0, 1, i)
            scores(3)
            gate_u(0, 0)
            gate_u(0, 1)
            gate_w(0, 1, 4)
            h_turn(2)
            gate_u(0, 2)
            gate_w(0, 1, 5)
            probs_turn(3)
            gate_u(0, 3)
            attend(3)
            gate_u(0, 4)
            gate_u(0, 5)
            for i in range(3):
                gate_w(1, 0, i)
            h_turn(3)
            for i in range(3, 6):
                gate_w(1, 0, i)
            for g in range(GROUPS):
                if g == 1:
                    for i in range(4):
                        gate_w(1, 1, i)
                    gate_u(1, 0)
                    gate_u(1, 1)
                    gate_w(1, 1, 4)
                    gate_u(1, 2)
                    gate_w(1, 1, 5)
                    for i in range(3, 6):
                        gate_u(1, i)
                for j in range(TILES):
                    head_w(g, j)
                for j in range(TILES):
                    head_c_part(g, j)


def kernel(**inputs):
    import numpy as np
    import concourse.bacc as bacc
    from concourse.bass_utils import run_bass_kernel_spmd

    def rows(name):
        return np.asarray(inputs[name])

    def chunks(a):
        return a.reshape(KC, P, -1).transpose(1, 0, 2)

    x = rows("x")
    xT = x.reshape(STEPS, GROUPS, P, TILES, KC, P).transpose(5, 1, 0, 4, 3, 2).reshape(P, SLABS, KC, SLAB)
    ctx_w = np.concatenate([chunks(rows("L0_xattn_W").T), chunks(rows("ctx_1024").reshape(-1, D).T)], axis=2)
    wT = np.stack([chunks(rows("L0_ffn_" + n).T) for n in ("wf", "wi", "wc", "wo")], axis=2)
    uT = np.stack([chunks(rows("L0_ffn_" + n).T) for n in ("uf", "ui", "uc", "uo")], axis=2)
    vecs = np.concatenate([rows(n).reshape(KC, P).T for n in
                           ("L0_ffn_bf", "L0_ffn_bi", "L0_ffn_bc", "L0_xattn_b", "L0_ffn_in_c")], axis=1)
    arrays = {"x": x, "xT": xT, "ctx_w": ctx_w, "wT": wT, "uT": uT, "vecs": vecs,
              "bo": rows("L0_ffn_bo").reshape(1, D)}
    arrays = {n: np.ascontiguousarray(a) for n, a in arrays.items()}

    nc = bacc.Bacc("TRN2", target_bir_lowering=False, num_devices=1)
    aps = {n: nc.dram_tensor(n, a.shape, F32, kind="ExternalInput").ap() for n, a in arrays.items()}
    out = nc.dram_tensor("out", x.shape, F32, kind="ExternalOutput").ap()
    build(nc, out=out, **aps)
    r = run_bass_kernel_spmd(nc, [arrays], core_ids=[0])
    return r.results[0]["out"]
```

```python
from contextlib import ExitStack

import concourse.bass as bass
from concourse import mybir

F32 = mybir.dt.float32
F32R = mybir.dt.float32r
ALU = mybir.AluOpType
ACT = mybir.ActivationFunctionType
AX = mybir.AxisListType

P = 128
STEPS, ROWS, D = 2, 1024, 256
KEYS = 77
KC = D // P
GROUPS = 2
SLAB = ROWS // GROUPS
TILES = SLAB // P
SLABS = GROUPS * STEPS
EPS = 1e-5
GATES = 3
HEAD = 3
RING = 4
CW_COLS = D + STEPS * KEYS
V_GATE, V_ATTN, V_C0, V_COUNT = 0, GATES * KC, GATES * KC + KC, GATES * KC + 2 * KC


def build(nc, x, xT, vec_cw, wT, uT, bo, out):
    with ExitStack() as ctx:
        def sb(name, shape, dt=F32):
            return ctx.enter_context(nc.sbuf_tensor(name, shape, dt))

        def psum(name):
            return ctx.enter_context(nc.psum_tensor(name, [P, 512], F32))

        def sem(name):
            return ctx.enter_context(nc.semaphore(name))

        X = sb("X", [P, SLABS, TILES, D])
        XT = sb("XT", [P, 2, KC, SLAB])
        vec_CW = sb("vec_CW", [P, V_COUNT + KC * CW_COLS])
        vec = vec_CW[:, 0:V_COUNT]
        CW = vec_CW[:, V_COUNT:].rearrange("p (k c) -> p k c", k=KC)
        W = sb("W", [P, KC, HEAD + 1, D])
        U = sb("U", [P, KC, HEAD + 1, D])
        W_hi = sb("W_hi", [P, KC, HEAD + 1, D], F32R)
        W_lo = sb("W_lo", [P, KC, HEAD + 1, D], F32R)
        U_hi = sb("U_hi", [P, KC, HEAD + 1, D], F32R)
        U_lo = sb("U_lo", [P, KC, HEAD + 1, D], F32R)
        bo_all = sb("bo_all", [P, D])
        ident = sb("ident", [P, P])
        mean_w = sb("mean_w", [P, P])
        neg_half = sb("neg_half", [P, TILES])
        T_T = sb("T_T", [P, KC, STEPS * KEYS])
        Tc_T = sb("Tc_T", [P, KC, STEPS * KEYS])
        w_stats = sb("w_stats", [P, KC, 6])
        w_mean = sb("w_mean", [P, KC, 2])
        W_c = sb("W_c", [P, KC, D])
        b_c = sb("b_c", [P, KC])
        T_rows = sb("T_rows", [KEYS, STEPS, D])
        T_hi = sb("T_hi", [KEYS, STEPS, D], F32R)
        T_lo = sb("T_lo", [KEYS, STEPS, D], F32R)
        bias0 = sb("bias0", [P, GATES * KC])
        bias1 = sb("bias1", [P, GATES * KC])
        bias_u = sb("bias_u", [P, GATES * KC])
        st1 = sb("st1", [P, SLABS, TILES, 6])
        mv1 = sb("mv1", [P, SLABS, TILES, 2])
        ve1 = sb("ve1", [P, SLABS, TILES])
        rstd1 = sb("rstd1", [P, SLABS, TILES])
        st2 = sb("st2", [P, SLABS, TILES, 6])
        mv2 = sb("mv2", [P, SLABS, TILES, 2])
        ve2 = sb("ve2", [P, SLABS, TILES])
        rstd2 = sb("rstd2", [P, SLABS, TILES])
        row_max = sb("row_max", [P, SLABS, TILES])
        exp_bias = sb("exp_bias", [P, SLABS, TILES])
        row_sum = sb("row_sum", [P, SLABS, TILES])
        row_rec = sb("row_rec", [P, SLABS, TILES])
        probs = sb("probs", [P, SLABS, TILES, KEYS])
        probs_n = sb("probs_n", [P, SLABS, TILES, KEYS])
        probs_T = sb("probs_T", [KEYS, STEPS, SLAB])
        probs_T_hi = sb("probs_T_hi", [KEYS, STEPS, SLAB], F32R)
        probs_T_lo = sb("probs_T_lo", [KEYS, STEPS, SLAB], F32R)
        H = sb("H", [P, 2, TILES, D])
        HT_hi = sb("HT_hi", [P, SLABS, KC, SLAB], F32R)
        HT_lo = sb("HT_lo", [P, SLABS, KC, SLAB], F32R)
        gate = sb("gate", [P, GATES, KC, SLAB])
        keep = sb("keep", [P, KC, SLAB])
        add = sb("add", [P, KC, SLAB])
        C = sb("C", [P, 2, KC, SLAB])
        C_hi = sb("C_hi", [P, 2, KC, SLAB], F32R)
        C_lo = sb("C_lo", [P, 2, KC, SLAB], F32R)
        c_head = sb("c_head", [P, D])
        head = sb("head", [P, TILES, STEPS, D])
        warm = sb("warm", [P, 1])

        p_scores = psum("p_scores")
        p_probsT = psum("p_probsT")
        p_slab = [psum(f"p_slab{k}") for k in range(2)]
        p_ring = [psum(f"p_ring{k}") for k in range(RING)]
        p_head_c = [p_scores, p_probsT, *p_slab]
        p_last = p_scores
        p_t = (p_slab[1], p_ring[2])
        p_tc = (p_probsT, p_slab[0])
        p_bmean = p_ring[1]

        def p_score(s, a):
            return p_ring[0] if s == 1 else p_ring[3] if (s, a) == (0, 2) else p_scores

        def p_turn(s, a):
            return p_ring[2] if (s, a) == (0, 2) else p_probsT

        def p_att(s):
            return p_ring[2:4] if s == 1 else p_slab

        def p_hT(s, a):
            return p_ring[2:4] if (s, a) == (0, 2) else p_slab

        def parts(s):
            return ((0, 2), (2, TILES)) if s == 0 else ((0, TILES),)

        def quarters(s, a, k):
            return KC * (a // 2) + k + 1 if s == 0 else 2 * KC * s + 2 * (k + 1)

        l_bo, l_w, l_u, l_wo, l_uo = (sem(n) for n in ("l_bo", "l_w", "l_u", "l_wo", "l_uo"))
        l_cw = [sem(f"l_cw{k}") for k in range(KC)]
        l_x = {(s, a): sem(f"l_x{s}_{a}") for s in range(SLABS) for a, _ in parts(s)}
        l_xT = {(s, a): sem(f"l_xT{s}_{a}") for s in range(SLABS) for a, _ in parts(s)}
        stored = [sem(f"stored{j}") for j in range(TILES)]
        s_warm = sem("s_warm")
        s_zero = sem("s_zero")
        s_ident = sem("s_ident")
        s_half = sem("s_half")
        s_mean = sem("s_mean")
        s_whi = sem("s_whi")
        s_wlo = sem("s_wlo")
        s_head_hi = sem("s_head_hi")
        s_head_lo = sem("s_head_lo")
        s_uhi = sem("s_uhi")
        s_ulo = sem("s_ulo")
        s_wst = sem("s_wst")
        s_wmean = sem("s_wmean")
        s_bmean = sem("s_bmean")
        s_bc = sem("s_bc")
        s_tps = sem("s_tps")
        s_tT = sem("s_tT")
        s_wc = sem("s_wc")
        s_tcps = sem("s_tcps")
        s_trows = sem("s_trows")
        s_tc = sem("s_tc")
        s_trc = sem("s_trc")
        s_thi = sem("s_thi")
        s_tlo = sem("s_tlo")
        s_bps = sem("s_bps")
        s_bu = sem("s_bu")
        s_bias = sem("s_bias")
        s_st1, s_mv1, s_ve1, s_rstd1 = (sem(n) for n in ("s_st1", "s_mv1", "s_ve1", "s_rstd1"))
        s_scores = sem("s_scores")
        s_max = sem("s_max")
        s_ebias = sem("s_ebias")
        s_exp = sem("s_exp")
        s_rec = sem("s_rec")
        s_pn = sem("s_pn")
        s_pT = sem("s_pT")
        s_pTc = sem("s_pTc")
        s_pTlo = sem("s_pTlo")
        s_att = sem("s_att")
        s_x1 = sem("s_x1")
        s_st2, s_mv2, s_ve2, s_rstd2 = (sem(n) for n in ("s_st2", "s_mv2", "s_ve2", "s_rstd2"))
        s_h = sem("s_h")
        s_hT = sem("s_hT")
        s_hhi = sem("s_hhi")
        s_hlo = sem("s_hlo")
        s_ring = sem("s_ring")
        s_act = sem("s_act")
        s_keep = sem("s_keep")
        s_add = sem("s_add")
        s_c = sem("s_c")
        s_chi = sem("s_chi")
        s_clo = sem("s_clo")
        s_hc = sem("s_hc")
        s_hb = sem("s_hb")
        s_last = sem("s_last")
        s_ch = sem("s_ch")
        s_pre = sem("s_pre")
        s_tanh = sem("s_tanh")
        s_y = [sem("s_y_pool"), sem("s_y_dve")]

        first = {("gates", 0, 0): 0, ("gates", 0, 1): 6, ("gates", 1, 0): 12, ("head", 0): 18,
                 ("gates", 1, 1): 22, ("head", 1): 28}

        def taken(n):
            return n + 1 - TILES * sum(first["head", g] < n for g in range(GROUPS))

        def steps_of(j):
            return ((0, 1), (1, 2)) if j == TILES - 1 else ((0, STEPS),)

        def halves(g, j, t=STEPS - 1):
            return 2 * (TILES * g + j) + t + 1

        def halves_y(g, j, t=STEPS - 1):
            return 4 * g + 2 * (j // 2) + t + 1

        def gate_of(i):
            return i // GATES, i % GATES

        block = ctx.enter_context(nc.Block())

        @block.sync
        def _(sp):
            n = V_COUNT + CW_COLS
            sp.dma_start(vec_CW[:, 0:n], vec_cw[:, 0:n]).then_inc(l_cw[0], 16)
            sp.dma_start(vec_CW[:, n:], vec_cw[:, n:]).then_inc(l_cw[1], 16)

            def load_slab(s):
                if s >= 2:
                    sp.wait_ge(s_scores, TILES * (s - 1))
                for a, b in parts(s):
                    g, t = s // STEPS, s % STEPS
                    rows = x[t, g * SLAB:(g + 1) * SLAB, :].rearrange("(p j) d -> p j d", j=TILES)
                    sp.dma_start(X[:, s, a:b], rows[:, a:b]).then_inc(l_x[s, a], 16)
                    if s == 1:
                        sp.dma_start(W[:, :, 0:GATES], wT[:, :, 0:GATES]).then_inc(l_w, 16)
                    sp.dma_start(XT[:, s % 2, :, a * P:b * P], xT[:, s, :, a * P:b * P]).then_inc(l_xT[s, a], 16)

            load_slab(0)
            sp.dma_start(U[:, :, 0:GATES], uT[:, :, 0:GATES]).then_inc(l_u, 16)
            load_slab(1)
            load_slab(2)
            sp.dma_start(U[:, :, HEAD], uT[:, :, HEAD]).then_inc(l_uo, 16)
            sp.dma_start(W[:, :, HEAD], wT[:, :, HEAD]).then_inc(l_wo, 16)
            sp.dma_start(bo_all[:], bo.to_broadcast([P, D])).then_inc(l_bo, 16)
            load_slab(3)
            for g in range(GROUPS):
                for j in range(TILES):
                    rows = out[:, g * SLAB:(g + 1) * SLAB, :].rearrange("t (p j) d -> p j t d", j=TILES)
                    for a, b in steps_of(j):
                        sp.wait_ge(s_y[j % 2], halves_y(g, j, b - 1))
                        sp.dma_start(rows[:, j, a:b], X[:, STEPS * g + a:STEPS * g + b, j]).then_inc(stored[j], 16)
            for j in range(TILES):
                sp.wait_ge(stored[j], 16 * GROUPS * len(steps_of(j)))

        @block.gpsimd
        def _(pool):
            nc.gpsimd.memset(ident[:], 0.0).then_inc(s_zero, 1)
            pool.wait_ge(s_zero, 1)
            nc.gpsimd.affine_select(out=ident[:], in_=ident[:], compare_op=ALU.not_equal, fill=1.0, base=0,
                                    pattern=[[-1, P]], channel_multiplier=1).then_inc(s_ident, 1)
            nc.gpsimd.memset(neg_half[:], -0.5).then_inc(s_half, 1)
            pool.wait_ge(s_half, 1)

            def deviation1(s):
                for a, b in parts(s):
                    pool.wait_ge(s_mv1, TILES * s + b)
                    nc.gpsimd.tensor_scalar(ve1[:, s, a:b], mv1[:, s, a:b, 1], EPS, 1.0, ALU.add,
                                            ALU.mult).then_inc(s_ve1, b - a)
                    pool.wait_ge(s_ve1, TILES * s + b)
                    nc.gpsimd.tensor_tensor(rstd1[:, s, a:b], ve1[:, s, a:b], neg_half[:, a:b],
                                            ALU.pow).then_inc(s_rstd1, b - a)

            def deviation2(s, which=None):
                for a, b in (which,) if which else parts(s):
                    pool.wait_ge(s_mv2, TILES * s + b)
                    nc.gpsimd.tensor_scalar(ve2[:, s, a:b], mv2[:, s, a:b, 1], EPS, 1.0, ALU.add,
                                            ALU.mult).then_inc(s_ve2, b - a)
                    pool.wait_ge(s_ve2, TILES * s + b)
                    nc.gpsimd.tensor_tensor(rstd2[:, s, a:b], ve2[:, s, a:b], neg_half[:, a:b],
                                            ALU.pow).then_inc(s_rstd2, b - a)

            def lo(w_lo, w, w_hi, ready, count, done):
                pool.wait_ge(ready, count)
                nc.gpsimd.tensor_tensor(w_lo, w, w_hi.bitcast(F32), ALU.subtract).then_inc(done, 1)

            def w_lo(k, q):
                lo(W_lo[:, k, q], W[:, k, q], W_hi[:, k, q], s_whi, k + 1, s_wlo)

            def u_lo(k):
                lo(U_lo[:, k, 0:GATES], U[:, k, 0:GATES], U_hi[:, k, 0:GATES], s_uhi, k + 1, s_ulo)

            def output(g, j):
                pool.wait_ge(s_tanh, halves(g, j))
                x1 = X[:, STEPS * g:STEPS * (g + 1), j]
                nc.gpsimd.tensor_tensor(x1, head[:, j], x1, ALU.add).then_inc(s_y[0], 2)

            deviation1(0)
            deviation1(1)
            deviation2(0)
            w_lo(0, 0)
            w_lo(1, 0)
            for q in range(1, GATES):
                for k in range(KC):
                    w_lo(k, q)
            pool.wait_ge(s_thi, 1)
            nc.gpsimd.tensor_tensor(T_lo[:], T_rows[:], T_hi[:].bitcast(F32), ALU.subtract).then_inc(s_tlo, 1)
            deviation1(2)
            deviation2(1, (0, 2))
            deviation2(1, (2, 4))
            u_lo(0)
            u_lo(1)
            deviation2(2)
            deviation1(3)
            lo(W_lo[:, :, HEAD], W[:, :, HEAD], W_hi[:, :, HEAD], s_head_hi, 1, s_head_lo)
            lo(U_lo[:, :, HEAD], U[:, :, HEAD], U_hi[:, :, HEAD], s_head_hi, 2, s_head_lo)
            deviation2(3)
            for g in range(GROUPS):
                for j in range(0, TILES, 2):
                    output(g, j)

        @block.scalar
        def _(act):
            act.wait_ge(s_warm, 1)
            nc.scalar.activation(warm[:], warm[:], ACT.Exp).then_inc(s_warm, 1)

            def exponentials(s, first_j=0, end_j=TILES):
                for a, b in parts(s):
                    a, b = max(a, first_j), min(b, end_j)
                    if a >= b:
                        continue
                    act.wait_ge(s_ebias, TILES * s + (b if s == 0 else TILES))
                    for j in range(a, b):
                        e = nc.scalar.activation(probs[:, s, j], p_score(s, a)[:, j * KEYS:(j + 1) * KEYS], ACT.Exp,
                                                 bias=exp_bias[:, s, j:j + 1], scale=rstd1[:, s, j:j + 1],
                                                 accum_out=row_sum[:, s, j:j + 1])
                        e.then_inc(s_exp, 1)

            def probs_T_copy(s, which=None):
                for a, b in (which,) if which else parts(s):
                    act.wait_ge(s_pT, TILES * s + b)
                    to = (probs_T, probs_T_hi)[s // STEPS]
                    rows = slice(a * P, b * P)
                    nc.scalar.copy(to[:, s % STEPS, rows], p_turn(s, a)[0:KEYS, rows]).then_inc(s_pTc, b - a)

            def h_hi(s, which=None):
                for a, b in (which,) if which else parts(s):
                    for k in range(KC):
                        act.wait_ge(s_hT, quarters(s, a, k))
                        rows = slice(a * P, b * P)
                        nc.scalar.copy(HT_hi[:, s, k, rows], p_hT(s, a)[k][:, rows]).then_inc(s_hhi, (b - a) // 2)

            def gate_tanh(g, t, i):
                n = first["gates", g, t] + i
                oc, q = gate_of(i)
                act.wait_ge(s_ring, n + 1)
                if (t, i) == (0, 0):
                    act.wait_ge(s_bias, 4)
                if (g, t) != (0, 0):
                    act.wait_ge(s_keep, 4 * g + 2 * t + oc - 1)
                    act.wait_ge(s_add, 4 * g + 2 * t + oc - 1)
                bias = (bias0, bias1)[t]
                c = q * KC + oc
                nc.scalar.activation(gate[:, q, oc], p_ring[n % RING][:], ACT.Tanh, bias=bias[:, c:c + 1],
                                     scale=1.0 if q == 2 else 0.5).then_inc(s_act, 1)

            def c_hi(g, t, oc):
                act.wait_ge(s_c, 4 * g + 2 * t + oc + 1)
                if g == 1 and t == 0:
                    act.wait_ge(s_ring, 12)
                if g == 1 and t == 1:
                    act.wait_ge(s_hc, TILES)
                nc.scalar.mul(C_hi[:, t, oc], C[:, t, oc], 0.5).then_inc(s_chi, 1)

            def head_tanh(g, j):
                for a, b in steps_of(j):
                    act.wait_ge(s_pre, halves(g, j, b - 1))
                    nc.scalar.activation(head[:, j, a:b], head[:, j, a:b], ACT.Tanh).then_inc(s_tanh, b - a)

            def w_hi(k):
                act.wait_ge(l_w, 16)
                nc.scalar.copy(W_hi[:, k, 0:GATES], W[:, k, 0:GATES]).then_inc(s_whi, 1)

            def u_hi(k):
                act.wait_ge(l_u, 16)
                nc.scalar.copy(U_hi[:, k, 0:GATES], U[:, k, 0:GATES]).then_inc(s_uhi, 1)

            act.wait_ge(s_tps, KC)
            for oc in range(KC):
                nc.scalar.add(T_T[:, oc], p_t[oc][:, 0:STEPS * KEYS],
                              vec[:, V_ATTN + oc:V_ATTN + oc + 1]).then_inc(s_tT, 1)
            exponentials(0)
            act.wait_ge(s_trows, 1)
            nc.scalar.copy(T_rows[:], p_slab[0][0:KEYS, :].rearrange("p (t d) -> p t d", t=STEPS)).then_inc(s_trc, 1)
            probs_T_copy(0, (0, 2))
            probs_T_copy(0, (2, 4))
            w_hi(0)
            w_hi(1)
            u_hi(0)
            act.wait_ge(s_trc, 1)
            nc.scalar.copy(T_hi[:], T_rows[:]).then_inc(s_thi, 1)
            h_hi(0, (0, 2))
            exponentials(1)
            probs_T_copy(1)
            u_hi(1)
            gate_tanh(0, 0, 0)
            gate_tanh(0, 0, 1)
            exponentials(2)
            gate_tanh(0, 0, 2)
            gate_tanh(0, 0, 3)
            h_hi(1)
            probs_T_copy(2)
            gate_tanh(0, 0, 4)
            gate_tanh(0, 0, 5)
            c_hi(0, 0, 0)
            c_hi(0, 0, 1)
            act.wait_ge(l_wo, 16)
            nc.scalar.copy(W_hi[:, :, HEAD], W[:, :, HEAD]).then_inc(s_head_hi, 1)
            act.wait_ge(l_uo, 16)
            nc.scalar.copy(U_hi[:, :, HEAD], U[:, :, HEAD]).then_inc(s_head_hi, 1)
            gate_tanh(0, 1, 0)
            exponentials(3, 0, 2)
            gate_tanh(0, 1, 1)
            exponentials(3, 2, 4)
            h_hi(2)
            gate_tanh(0, 1, 2)
            probs_T_copy(3)
            gate_tanh(0, 1, 3)
            c_hi(0, 1, 0)
            gate_tanh(0, 1, 4)
            gate_tanh(0, 1, 5)
            gate_tanh(1, 0, 0)
            c_hi(0, 1, 1)
            for i in range(1, 4):
                gate_tanh(1, 0, i)
            c_hi(1, 0, 0)
            gate_tanh(1, 0, 4)
            h_hi(3)
            gate_tanh(1, 0, 5)
            for j in range(TILES):
                head_tanh(0, j)
            c_hi(1, 0, 1)
            for i in range(5):
                gate_tanh(1, 1, i)
            c_hi(1, 1, 0)
            gate_tanh(1, 1, 5)
            c_hi(1, 1, 1)
            for j in range(TILES):
                head_tanh(1, j)

        @block.vector
        def _(dve):
            nc.vector.memset(warm[:], 0.0).then_inc(s_warm, 1)
            nc.vector.memset(mean_w[:], 1.0 / D).then_inc(s_mean, 1)

            def stats1(s, a=0, b=TILES):
                sums1(s, a, b)
                variances1(s, a, b)

            def sums1(s, a, b):
                dve.wait_ge(l_x[s, a if s == 0 else 0], 16)
                for j in range(a, b):
                    nc.vector.bn_stats(st1[:, s, j], X[:, s, j]).then_inc(s_st1, 1)

            def variances1(s, a, b):
                for j in range(a, b):
                    dve.wait_ge(s_st1, TILES * s + j + 1)
                    nc.vector.bn_aggr(mv1[:, s, j], st1[:, s, j]).then_inc(s_mv1, 1)

            def score_max(s, which=None):
                for a, b in (which,) if which else parts(s):
                    dve.wait_ge(s_scores, TILES * s + b)
                    scores = p_score(s, a)[:, a * KEYS:b * KEYS].rearrange("p (j k) -> p j k", j=b - a)
                    nc.vector.tensor_reduce(row_max[:, s, a:b], scores, AX.X, ALU.max).then_inc(s_max, b - a)

            def max_scaled(s, which=None):
                for a, b in (which,) if which else parts(s):
                    dve.wait_ge(s_max, TILES * s + b)
                    dve.wait_ge(s_rstd1, TILES * s + b)
                    nc.vector.scalar_tensor_tensor(exp_bias[:, s, a:b], row_max[:, s, a:b], -1.0, rstd1[:, s, a:b],
                                                   ALU.mult, ALU.mult).then_inc(s_ebias, b - a)

            def normalise(s, a=0, b=TILES):
                dve.wait_ge(s_exp, TILES * s + b)
                nc.vector.reciprocal(row_rec[:, s, a:b], row_sum[:, s, a:b]).then_inc(s_rec, b - a)
                dve.wait_ge(s_rec, TILES * s + b)
                rec = row_rec[:, s, a:b].unsqueeze(2).to_broadcast([P, b - a, KEYS])
                nc.vector.tensor_tensor(probs_n[:, s, a:b], probs[:, s, a:b], rec, ALU.mult).then_inc(s_pn, b - a)

            def probs_lo(s):
                dve.wait_ge(s_pTc, TILES * (s + 1))
                nc.vector.tensor_tensor(probs_T_lo[:, s % STEPS], p_turn(s, 0)[0:KEYS, :],
                                        probs_T_hi[:, s % STEPS].bitcast(F32), ALU.subtract).then_inc(s_pTlo, 1)

            def residual(s, i):
                dve.wait_ge(s_att, 2 * s + i + 1)
                x_rows = X[:, s, 2 * i:2 * i + 2]
                attention = p_att(s)[i][:].rearrange("p (j d) -> p j d", j=2)
                nc.vector.scalar_tensor_tensor(x_rows, attention, 0.0, x_rows, ALU.max, ALU.add).then_inc(s_x1, 1)

            def stats2(s, i):
                dve.wait_ge(s_x1, 2 * s + i + 1)
                for j in (2 * i, 2 * i + 1):
                    nc.vector.bn_stats(st2[:, s, j], X[:, s, j]).then_inc(s_st2, 1)
                for j in (2 * i, 2 * i + 1):
                    dve.wait_ge(s_st2, TILES * s + j + 1)
                    nc.vector.bn_aggr(mv2[:, s, j], st2[:, s, j]).then_inc(s_mv2, 1)

            def layernorm(s, which=None):
                if s >= 2:
                    dve.wait_ge(s_hT, 2 * KC * (s - 1))
                for a, b in (which,) if which else parts(s):
                    dve.wait_ge(s_rstd2, TILES * s + b)
                    for j in range(a, b):
                        nc.vector.tensor_scalar(H[:, s % 2, j], X[:, s, j], mv2[:, s, j, 0:1], rstd2[:, s, j:j + 1],
                                                ALU.subtract, ALU.mult).then_inc(s_h, 1)

            def h_lo(s, which=None):
                for a, b in (which,) if which else parts(s):
                    for k in range(KC):
                        dve.wait_ge(s_hhi, quarters(s, a, k))
                        c = slice(a * P, b * P)
                        hi = HT_hi[:, s, k, c].bitcast(F32)
                        nc.vector.tensor_tensor(HT_lo[:, s, k, c], p_hT(s, a)[k][:, c], hi,
                                                ALU.subtract).then_inc(s_hlo, (b - a) // 2)

            def state_keep(g, t, oc):
                done = 4 * g + 2 * t + oc
                dve.wait_ge(s_act, taken(first["gates", g, t] + GATES * oc))
                if done >= 2:
                    dve.wait_ge(s_c, done - 1)
                if t == 0:
                    nc.vector.tensor_scalar(keep[:, oc], gate[:, 0, oc], 1.0, vec[:, V_C0 + oc:V_C0 + oc + 1],
                                            ALU.add, ALU.mult).then_inc(s_keep, 1)
                else:
                    nc.vector.scalar_tensor_tensor(keep[:, oc], gate[:, 0, oc], 1.0, C[:, 0, oc],
                                                   ALU.add, ALU.mult).then_inc(s_keep, 1)

            def state_add(g, t, oc):
                done = 4 * g + 2 * t + oc
                dve.wait_ge(s_act, taken(first["gates", g, t] + GATES * oc + GATES - 1))
                if done >= 2:
                    dve.wait_ge(s_c, done - 1)
                nc.vector.scalar_tensor_tensor(add[:, oc], gate[:, 1, oc], 1.0, gate[:, 2, oc],
                                               ALU.add, ALU.mult).then_inc(s_add, 1)

            def state_sum(g, t, oc):
                done = 4 * g + 2 * t + oc
                dve.wait_ge(s_keep, done + 1)
                dve.wait_ge(s_add, done + 1)
                if g == 1:
                    dve.wait_ge(s_clo, 2 * t + oc + 1)
                nc.vector.scalar_tensor_tensor(C[:, t, oc], keep[:, oc], (1.0, 0.5)[t], add[:, oc],
                                               ALU.mult, ALU.add).then_inc(s_c, 1)

            def state(g, t, oc):
                state_keep(g, t, oc)
                state_add(g, t, oc)
                state_sum(g, t, oc)

            def c_lo(g, t, oc):
                dve.wait_ge(s_chi, 4 * g + 2 * t + oc + 1)
                nc.vector.scalar_tensor_tensor(C_lo[:, t, oc], C[:, t, oc], 0.5, C_hi[:, t, oc].bitcast(F32),
                                               ALU.mult, ALU.subtract).then_inc(s_clo, 1)

            def head_bias(g, j):
                if (g, j) == (0, 0):
                    dve.wait_ge(l_bo, 16)
                n = first["head", g] + j
                dve.wait_ge(s_ring, n + 1)
                if g == 1:
                    dve.wait_ge(s_y[j % 2], halves_y(0, j))
                b = bo_all[:].unsqueeze(1).to_broadcast([P, STEPS, D])
                nc.vector.tensor_tensor(head[:, j], p_ring[n % RING][:].rearrange("p (t d) -> p t d", t=STEPS), b,
                                        ALU.add).then_inc(s_hb, 1)

            def head_sum(g, j):
                dve.wait_ge(s_hc, TILES * g + j + 1)
                dve.wait_ge(s_hb, (TILES - 1) * g + j + 1)
                c = p_head_c[j][:, 0:D].unsqueeze(1).to_broadcast([P, STEPS, D])
                nc.vector.tensor_tensor(head[:, j], head[:, j], c, ALU.add).then_inc(s_pre, 2)

            def last_c(g):
                dve.wait_ge(s_hc, TILES * (g + 1))
                nc.vector.tensor_tensor(c_head[:], p_head_c[TILES - 1][:, 0:D], bo_all[:], ALU.add).then_inc(s_ch, 1)
                if g == 1:
                    dve.wait_ge(s_y[1], halves_y(0, TILES - 1))

            def last_sum(g, t):
                n = first["head", g] + TILES - 1
                if t == 0:
                    dve.wait_ge(s_ring, n + 1)
                    dve.wait_ge(s_ch, g + 1)
                else:
                    dve.wait_ge(s_last, g + 1)
                bank = p_ring[n % RING] if t == 0 else p_last
                nc.vector.tensor_tensor(head[:, TILES - 1, t], bank[:, 0:D], c_head[:], ALU.add).then_inc(s_pre, 1)

            def output(g, j, a=0, b=STEPS):
                dve.wait_ge(s_tanh, halves(g, j, b - 1))
                x1 = X[:, STEPS * g + a:STEPS * g + b, j]
                nc.vector.tensor_tensor(x1, head[:, j, a:b], x1, ALU.add).then_inc(s_y[1], b - a)

            for k in range(KC):
                dve.wait_ge(l_cw[k], 16)
                nc.vector.bn_stats(w_stats[:, k], CW[:, k, 0:D]).then_inc(s_wst, 1)
            for k in range(KC):
                dve.wait_ge(s_wst, k + 1)
                nc.vector.bn_aggr(w_mean[:, k], w_stats[:, k]).then_inc(s_wmean, 1)
            for k in range(KC):
                dve.wait_ge(s_wmean, k + 1)
                nc.vector.tensor_scalar(W_c[:, k], CW[:, k, 0:D], w_mean[:, k, 0:1], None,
                                        ALU.subtract).then_inc(s_wc, 1)
            dve.wait_ge(s_bmean, 1)
            nc.vector.tensor_tensor(b_c[:], vec[:, V_ATTN:V_ATTN + KC], p_bmean[:, 0:1].to_broadcast([P, KC]),
                                    ALU.subtract).then_inc(s_bc, 1)
            sums1(0, 0, 2)
            for oc in range(KC):
                dve.wait_ge(s_tcps, oc + 1)
                dve.wait_ge(s_bc, 1)
                nc.vector.tensor_scalar(Tc_T[:, oc], p_tc[oc][:, 0:STEPS * KEYS], b_c[:, oc:oc + 1], None,
                                        ALU.add).then_inc(s_tc, 1)
            variances1(0, 0, 2)
            stats1(0, 2, TILES)
            for part in parts(0):
                score_max(0, part)
                max_scaled(0, part)
            normalise(0, 0, 2)
            normalise(0, 2, TILES)
            stats1(1)
            residual(0, 0)
            stats2(0, 0)
            residual(0, 1)
            stats2(0, 1)
            layernorm(0, (0, 2))
            score_max(1)
            max_scaled(1)
            layernorm(0, (2, 4))
            h_lo(0, (0, 2))
            for k in range(KC):
                dve.wait_ge(s_hT, quarters(0, 2, k))
                nc.vector.tensor_copy(HT_hi[:, 0, k, 2 * P:], p_hT(0, 2)[k][:, 2 * P:]).then_inc(s_hhi, 1)
            normalise(1)
            h_lo(0, (2, 4))
            n = 2 * KC
            nc.vector.tensor_scalar(bias1[:, 0:n], vec[:, 0:n], 0.5, None, ALU.mult).then_inc(s_bias, 1)
            nc.vector.tensor_copy(bias1[:, n:], vec[:, n:n + KC]).then_inc(s_bias, 1)
            dve.wait_ge(s_bps, KC * GATES)
            nc.vector.tensor_tensor(bias_u[:], p_ring[1][:, 0:GATES * KC], vec[:, 0:GATES * KC],
                                    ALU.add).then_inc(s_bu, 1)
            dve.wait_ge(s_bu, 1)
            nc.vector.tensor_scalar(bias0[:, 0:n], bias_u[:, 0:n], 0.5, None, ALU.mult).then_inc(s_bias, 1)
            nc.vector.tensor_copy(bias0[:, n:], bias_u[:, n:]).then_inc(s_bias, 1)
            stats1(2)
            score_max(2)
            residual(1, 0)
            max_scaled(2)
            residual(1, 1)
            stats2(1, 0)
            stats2(1, 1)
            normalise(2)
            layernorm(1, (0, 2))
            layernorm(1, (2, 4))
            h_lo(1)
            probs_lo(2)
            state_keep(0, 0, 0)
            state_add(0, 0, 0)
            state_keep(0, 0, 1)
            state_sum(0, 0, 0)
            state_add(0, 0, 1)
            residual(2, 0)
            state_sum(0, 0, 1)
            residual(2, 1)
            c_lo(0, 0, 0)
            c_lo(0, 0, 1)
            stats2(2, 0)
            stats2(2, 1)
            stats1(3)
            layernorm(2)
            score_max(3)
            max_scaled(3)
            normalise(3)
            h_lo(2)
            probs_lo(3)
            state(0, 1, 0)
            residual(3, 0)
            residual(3, 1)
            c_lo(0, 1, 0)
            stats2(3, 0)
            stats2(3, 1)
            state(0, 1, 1)
            layernorm(3)
            c_lo(0, 1, 1)
            state(1, 0, 0)
            c_lo(1, 0, 0)
            h_lo(3)
            for g in range(GROUPS):
                if g == 1:
                    state(1, 1, 0)
                    c_lo(1, 1, 0)
                    state(1, 1, 1)
                    head_bias(1, 0)
                    c_lo(1, 1, 1)
                else:
                    head_bias(0, 0)
                head_bias(g, 1)
                head_sum(g, 0)
                head_bias(g, 2)
                head_sum(g, 1)
                head_sum(g, 2)
                last_c(g)
                output(g, 1)
                last_sum(g, 0)
                last_sum(g, 1)
                if g == 0:
                    state(1, 0, 1)
                output(g, TILES - 1, 0, 1)
                output(g, TILES - 1, 1, 2)
                if g == 0:
                    c_lo(1, 0, 1)

        @block.tensor
        def _(pe):
            mm = nc.tensor.matmul

            def scores(s, a, b):
                t = s % STEPS
                pe.wait_ge(l_xT[s, a if s == 0 else 0], 16)
                pe.wait_ge(s_tc, KC)
                if s >= 2:
                    pe.wait_ge(s_exp, TILES * (2 * s - 3))
                for j in range(a, b):
                    for k in range(KC):
                        last = mm(p_score(s, a)[:, j * KEYS:(j + 1) * KEYS], XT[:, s % 2, k, j * P:(j + 1) * P],
                                  Tc_T[:, k, t * KEYS:(t + 1) * KEYS], start=(k == 0), stop=(k == KC - 1))
                last.then_inc(s_scores, b - a)

            def probs_turn(s, which=None):
                for a, b in (which,) if which else parts(s):
                    pe.wait_ge(s_pn, TILES * s + b)
                    if s >= 1:
                        pe.wait_ge(s_pTc, TILES * s)
                    if s == 3:
                        pe.wait_ge(s_pTlo, 1)
                    if (s, a) == (0, 2):
                        pe.wait_ge(s_tT, KC)
                    for j in range(a, b):
                        rows = slice(j * P, (j + 1) * P)
                        last = nc.tensor.transpose(p_turn(s, a)[0:KEYS, rows], probs_n[:, s, j], ident[:])
                    last.then_inc(s_pT, b - a)

            def attend(s):
                if s == 0:
                    pe.wait_ge(s_trc, 1)
                else:
                    pe.wait_ge(s_hlo, 2 * KC * s)
                for j in range(TILES):
                    if j % 2 == 0:
                        pe.wait_ge(s_pTc, TILES * s + (2 if (s, j) == (0, 0) else TILES))
                    t, rows = s % STEPS, slice(j * P, (j + 1) * P)
                    to = p_att(s)[j // 2][:, (j % 2) * D:(j % 2 + 1) * D]
                    if s < STEPS:
                        last = mm(to, probs_T[:, t, rows], T_rows[:, t], start=True, stop=True)
                    else:
                        pe.wait_ge(s_tlo, 1)
                        pe.wait_ge(s_pTlo, s - STEPS + 1)
                        mm(to, probs_T_hi[:, t, rows], T_hi[:, t], start=True, stop=False)
                        mm(to, probs_T_hi[:, t, rows], T_lo[:, t], start=False, stop=False)
                        last = mm(to, probs_T_lo[:, t, rows], T_hi[:, t], start=False, stop=True)
                    if j % 2:
                        last.then_inc(s_att, 1)

            def h_turn(s, which=None):
                if s == 1:
                    pe.wait_ge(s_hlo, 2 * KC)
                for a, b in (which,) if which else parts(s):
                    if (s, a) == (0, 0):
                        pe.wait_ge(s_x1, 2)
                    if (s, a) == (0, 2):
                        pe.wait_ge(s_pTc, TILES)
                        pe.wait_ge(s_exp, TILES)
                    pe.wait_ge(s_h, TILES * s + b)
                    for k in range(KC):
                        for j in range(a, b):
                            last = nc.tensor.transpose(p_hT(s, a)[k][:, j * P:(j + 1) * P],
                                                       H[:, s % 2, j, k * P:(k + 1) * P], ident[:])
                        last.then_inc(s_hT, (b - a) // 2)

            PASSES = ((0, 0), (1, 0), (0, 1))

            def wait_bank(n):
                for g in range(GROUPS):
                    j = n - RING - first["head", g]
                    if 0 <= j < TILES - 1:
                        pe.wait_ge(s_hb, (TILES - 1) * g + j + 1)
                        return
                    if j == TILES - 1:
                        pe.wait_ge(s_pre, halves(g, j, 0))
                        return
                if n >= RING:
                    pe.wait_ge(s_act, taken(n - RING))

            def gate_w(g, t, i):
                oc, q = gate_of(i)
                n = first["gates", g, t] + i
                s = STEPS * g + t
                if n == 0:
                    pe.wait_ge(s_exp, 2 * TILES)
                if n == 1:
                    pe.wait_ge(s_bu, 1)
                if n in (2, 3):
                    pe.wait_ge(s_x1, n + 1)
                wait_bank(n)
                for a, b in PASSES:
                    for k in range(KC):
                        if i == 0:
                            pe.wait_ge((s_hhi, s_hlo)[b], quarters(s, parts(s)[-1][0], k))
                        if n < GATES and a == 1:
                            pe.wait_ge(s_wlo, KC * q + k + 1)
                        last = mm(p_ring[n % RING][:], (W_hi, W_lo)[a][:, k, q, oc * P:(oc + 1) * P],
                                  (HT_hi, HT_lo)[b][:, s, k], start=((a, b, k) == (0, 0, 0)),
                                  stop=(t == 0 and b == 1 and k == KC - 1))
                if t == 0:
                    last.then_inc(s_ring, 1)

            def gate_u(g, i):
                oc, q = gate_of(i)
                n = first["gates", g, 1] + i
                if g == 0 and i == 0:
                    pe.wait_ge(s_ulo, KC)
                for a, b in PASSES:
                    for k in range(KC):
                        if i == 0:
                            pe.wait_ge((s_chi, s_clo)[b], 4 * g + k + 1)
                        last = mm(p_ring[n % RING][:], (U_hi, U_lo)[a][:, k, q, oc * P:(oc + 1) * P],
                                  (C_hi, C_lo)[b][:, 0, k], start=False, stop=(b == 1 and k == KC - 1))
                last.then_inc(s_ring, 1)

            def head_w(g, j):
                n = first["head", g] + j
                wait_bank(n)
                if (g, j) == (0, 0):
                    pe.wait_ge(s_head_lo, 2)
                for t in range(STEPS):
                    bank = p_ring[n % RING][:, t * D:(t + 1) * D]
                    if (j, t) == (TILES - 1, 1):
                        pe.wait_ge(s_pre, halves(g, 0))
                        bank = p_last[:, 0:D]
                    for a, b in PASSES:
                        for k in range(KC):
                            last = mm(bank,
                                      (HT_hi, HT_lo)[a][:, STEPS * g + t, k, j * P:(j + 1) * P],
                                      (W_hi, W_lo)[b][:, k, HEAD], start=((a, b, k) == (0, 0, 0)),
                                      stop=(b == 1 and k == KC - 1))
                    if j == TILES - 1:
                        last.then_inc((s_ring, s_last)[t], 1)
                if j < TILES - 1:
                    last.then_inc(s_ring, 1)

            def head_c_part(g, j):
                if g == 0:
                    pe.wait_ge(*((s_exp, TILES * SLABS), (s_pTlo, STEPS), (s_hlo, 2 * KC * SLABS),
                                 (s_hlo, 2 * KC * SLABS))[j])
                else:
                    pe.wait_ge(s_pre, halves(0, TILES - 1 if j == 0 else j))
                    if j == TILES - 1:
                        pe.wait_ge(s_ch, 1)
                for a, b in ((0, 0), (0, 1), (1, 0)):
                    for k in range(KC):
                        if j == 0:
                            pe.wait_ge((s_chi, s_clo)[a], 4 * g + 2 + k + 1)
                        last = mm(p_head_c[j][:, 0:D], (C_hi, C_lo)[a][:, 1, k, j * P:(j + 1) * P],
                                  (U_hi, U_lo)[b][:, k, HEAD], start=((a, b, k) == (0, 0, 0)),
                                  stop=(a == 1 and k == KC - 1))
                last.then_inc(s_hc, 1)

            def keep_warm(n, bank):
                ones = nc.const_aps.tensor(1.0, [P, P], mybir.dt.bfloat16)
                for _ in range(n):
                    mm(bank[:, 0:P], ones, ones, start=True, stop=True)

            def u_c0(oc, q, bank):
                pe.wait_ge(l_u, 16)
                c = q * KC + oc
                for k in range(KC):
                    last = mm(p_ring[1][:, c:c + 1], U[:, k, q, oc * P:(oc + 1) * P],
                              vec[:, V_C0 + k:V_C0 + k + 1], start=(k == 0), stop=(k == KC - 1))
                    keep_warm(1, bank)
                last.then_inc(s_bps, 1)

            def t_transposed(w, k, banks, done):
                for oc in range(KC):
                    last = mm(banks[oc][:, 0:STEPS * KEYS], w[:, k, oc * P:(oc + 1) * P], CW[:, k, D:],
                              start=(k == 0), stop=(k == KC - 1))
                    if k == KC - 1:
                        last.then_inc(done, 1)

            keep_warm(25, p_ring[0])
            pe.wait_ge(l_cw[0], 16)
            pe.wait_ge(s_mean, 1)
            for oc in range(KC):
                last = mm(p_bmean[:, 0:1], mean_w[:], vec[:, V_ATTN + oc:V_ATTN + oc + 1], start=(oc == 0),
                          stop=(oc == KC - 1))
            last.then_inc(s_bmean, 1)
            t_transposed(CW, 0, p_t, s_tps)
            for k in range(KC):
                pe.wait_ge(l_cw[k], 16)
                pe.wait_ge(s_wc, k + 1)
                t_transposed(W_c, k, p_tc, s_tcps)
            t_transposed(CW, 1, p_t, s_tps)
            scores(0, 0, 2)
            scores(0, 2, TILES)
            pe.wait_ge(s_ident, 1)
            pe.wait_ge(s_tT, KC)
            for t in range(STEPS):
                for oc in range(KC):
                    last = nc.tensor.transpose(p_slab[0][0:KEYS, t * D + oc * P:t * D + (oc + 1) * P],
                                               T_T[:, oc, t * KEYS:(t + 1) * KEYS], ident[:])
            last.then_inc(s_trows, 1)
            u_c0(0, 0, p_slab[1])
            u_c0(0, 1, p_slab[1])
            probs_turn(0, (0, 2))
            u_c0(0, 2, p_slab[1])
            probs_turn(0, (2, 4))
            attend(0)
            u_c0(1, 0, p_probsT)
            scores(1, 0, TILES)
            u_c0(1, 1, p_probsT)
            u_c0(1, 2, p_probsT)
            h_turn(0, (0, 2))
            scores(2, 0, 2)
            h_turn(0, (2, 4))
            scores(2, 2, 4)
            gate_w(0, 0, 0)
            probs_turn(1)
            gate_w(0, 0, 1)
            attend(1)
            for i in range(2, 5):
                gate_w(0, 0, i)
            probs_turn(2)
            h_turn(1)
            gate_w(0, 0, 5)
            gate_w(0, 1, 0)
            attend(2)
            for i in range(1, 4):
                gate_w(0, 1, i)
            scores(3, 0, TILES)
            gate_u(0, 0)
            gate_u(0, 1)
            gate_w(0, 1, 4)
            h_turn(2)
            gate_u(0, 2)
            gate_w(0, 1, 5)
            probs_turn(3)
            gate_u(0, 3)
            gate_u(0, 4)
            attend(3)
            gate_u(0, 5)
            for i in range(5):
                gate_w(1, 0, i)
            h_turn(3)
            gate_w(1, 0, 5)
            for g in range(GROUPS):
                if g == 1:
                    for i in range(4):
                        gate_w(1, 1, i)
                    gate_u(1, 0)
                    gate_u(1, 1)
                    gate_w(1, 1, 4)
                    gate_u(1, 2)
                    gate_w(1, 1, 5)
                    for i in range(3, 6):
                        gate_u(1, i)
                for j in range(TILES - 1):
                    head_w(g, j)
                for j in range(TILES):
                    head_c_part(g, j)
                head_w(g, TILES - 1)


def kernel(**inputs):
    import numpy as np
    import concourse.bacc as bacc
    from concourse.bass_utils import run_bass_kernel_spmd

    def rows(name):
        return np.asarray(inputs[name])

    def chunks(a):
        return a.reshape(KC, P, -1).transpose(1, 0, 2)

    x = rows("x")
    xT = x.reshape(STEPS, GROUPS, P, TILES, KC, P).transpose(5, 1, 0, 4, 3, 2).reshape(P, SLABS, KC, SLAB)
    wT = np.stack([chunks(rows("L0_ffn_" + n).T) for n in ("wf", "wi", "wc", "wo")], axis=2)
    uT = np.stack([chunks(rows("L0_ffn_" + n).T) for n in ("uf", "ui", "uc", "uo")], axis=2)
    vecs = np.concatenate([rows(n).reshape(KC, P).T for n in
                           ("L0_ffn_bf", "L0_ffn_bi", "L0_ffn_bc", "L0_xattn_b", "L0_ffn_in_c")], axis=1)
    w_ctx = np.concatenate([chunks(rows("L0_xattn_W").T), chunks(rows("ctx_1024").reshape(-1, D).T)], axis=2)
    vec_cw = np.concatenate([vecs, w_ctx.reshape(P, -1)], axis=1)
    arrays = {"x": x, "xT": xT, "vec_cw": vec_cw, "wT": wT, "uT": uT,
              "bo": rows("L0_ffn_bo").reshape(1, D)}
    arrays = {n: np.ascontiguousarray(a) for n, a in arrays.items()}

    nc = bacc.Bacc("TRN2", target_bir_lowering=False, num_devices=1)
    aps = {n: nc.dram_tensor(n, a.shape, F32, kind="ExternalInput").ap() for n, a in arrays.items()}
    out = nc.dram_tensor("out", x.shape, F32, kind="ExternalOutput").ap()
    build(nc, out=out, **aps)
    r = run_bass_kernel_spmd(nc, [arrays], core_ids=[0])
    return r.results[0]["out"]
```
